# Optimizing a Trainium2 kernel written in Bass

```python
import numpy as np
import jax
import jax.numpy as jnp

def _softmax(x, axis=-1):
    return jax.nn.softmax(x, axis=axis)

def _gelu(x):
    return jax.nn.gelu(x, approximate=True)

def _silu(x):
    return jax.nn.silu(x)

def _sigmoid(x):
    return jax.nn.sigmoid(x)

def _layernorm(x, axis=-1, eps=1e-05):
    m = jnp.mean(x, axis=axis, keepdims=True)
    v = jnp.var(x, axis=axis, keepdims=True)
    return (x - m) / jnp.sqrt(v + eps)

def _scatter_add(tgt, idx, src, axis=0):
    return tgt.at[idx].add(src)

def _segment_sum(src, seg, n):
    return jax.ops.segment_sum(src, seg, n)
kernel_name = 'mk_recurrent_d4_jaxref_r8_2ce68c'

def setup_inputs(seed: int=0):
    np.random.seed(seed)
    _w = jnp.asarray

    def _L0_attn_setup():
        import jax, jax.numpy as jnp
        import numpy as np
        B, T, C = (2, 256, 128)
        NH = 16
        HS = C // NH
        BD = max(HS // 4, 16)
        HORIZON = 32

        def _windows(t, delta):
            padded = jnp.pad(t, ((0, 0), (0, 0), (delta - 1, 0), (0, 0)))
            idx = jnp.arange(t.shape[2])[:, None] + jnp.arange(delta)[None, :]
            return padded[:, :, idx]
        key = jax.random.key(seed)
        ks = jax.random.split(key, 16)
        s = 0.02
        inp = {'x': jax.random.normal(ks[0], (B, T, C), dtype=jnp.float32), 'w_disp': jax.random.normal(ks[1], (C, NH * BD), dtype=jnp.float32) * s, 'b_disp': jnp.zeros((NH * BD,), dtype=jnp.float32), 'w_val': jax.random.normal(ks[2], (C, C), dtype=jnp.float32) * s, 'b_val': jnp.zeros((C,), dtype=jnp.float32), 'rel_pos_emb': jax.random.normal(ks[3], (HORIZON, BD), dtype=jnp.float32) * s, 'w_state': jax.random.normal(ks[4], (BD, BD), dtype=jnp.float32) * s, 'b_state': jnp.zeros((BD,), dtype=jnp.float32), 'w_strain': jax.random.normal(ks[5], (BD, BD), dtype=jnp.float32) * s, 'b_strain': jnp.zeros((BD,), dtype=jnp.float32), 'w_state_i': jax.random.normal(ks[6], (BD, BD), dtype=jnp.float32) * s, 'w_state_j': jax.random.normal(ks[7], (BD, BD), dtype=jnp.float32) * s, 'w_pos': jax.random.normal(ks[8], (BD, BD), dtype=jnp.float32) * s, 'w_bond_out': jax.random.normal(ks[9], (BD, 1), dtype=jnp.float32) * s, 'b_bond_out': jnp.zeros((1,), dtype=jnp.float32), 'w_damage': jax.random.normal(ks[10], (BD, BD), dtype=jnp.float32) * s, 'b_damage': jnp.zeros((BD,), dtype=jnp.float32), 'w_damage_out': jax.random.normal(ks[11], (BD, 1), dtype=jnp.float32) * s, 'b_damage_out': jnp.full((1,), -3.0, dtype=jnp.float32), 'w_cproj': jax.random.normal(ks[12], (C, C), dtype=jnp.float32) * s, 'b_cproj': jnp.zeros((C,), dtype=jnp.float32)}
        return inp
    _L0_attn_in = _L0_attn_setup()

    def _L0_ffn_setup():
        import jax, jax.numpy as jnp
        import numpy as np
        B, L, H = (32, 64, 128)
        E, R, TOP_K = (8, 16, 2)

        def _gates(cls, router_w):
            logits = jnp.einsum('bh,eh->be', cls, router_w)
            top_vals, top_idx = jax.lax.top_k(logits, TOP_K)
            mask = jnp.full_like(logits, -jnp.inf)
            rows = jnp.arange(logits.shape[0])[:, None]
            mask = mask.at[rows, top_idx].set(top_vals)
            return jax.nn.softmax(mask, axis=1)
        key = jax.random.key(seed)
        k1, k2, k3, k4 = jax.random.split(key, 4)
        x = jax.random.normal(k1, (B, L, H), dtype=jnp.float32)
        router_w = jax.random.normal(k2, (E, H), dtype=jnp.float32) * 0.02
        lora_down = jax.random.normal(k3, (E, R, H), dtype=jnp.float32) * (1.0 / np.sqrt(H))
        lora_up = jax.random.normal(k4, (E, H, R), dtype=jnp.float32) * (1.0 / np.sqrt(R))
        return {'x': x, 'router_w': router_w, 'lora_down': lora_down, 'lora_up': lora_up}
    _L0_ffn_in = _L0_ffn_setup()

    def _L1_attn_setup():
        import jax, jax.numpy as jnp
        import numpy as np
        B, T, E = (2, 512, 128)
        N_HEAD = 16
        HEAD_DIM = E // N_HEAD
        R = 4
        LD = E // 2
        HH = N_HEAD // 2

        def _split_heads(t, L):
            return t.reshape(t.shape[0], L, HH, HEAD_DIM).transpose(0, 2, 1, 3)

        def _causal_attn(q, k, v):
            L = q.shape[2]
            scores = jnp.einsum('bhqd,bhkd->bhqk', q, k) / jnp.sqrt(jnp.float32(HEAD_DIM))
            mask = jnp.tril(jnp.ones((L, L), dtype=bool))
            scores = jnp.where(mask, scores, -jnp.inf)
            att = jax.nn.softmax(scores, axis=-1)
            return jnp.einsum('bhqk,bhkd->bhqd', att, v)
        key = jax.random.key(seed)
        ks = jax.random.split(key, 14)
        s = 0.02

        def lin(k, din, dout):
            kw, kb = jax.random.split(k)
            return (jax.random.normal(kw, (din, dout), jnp.float32) * s, jax.random.normal(kb, (dout,), jnp.float32) * s)
        x = jax.random.normal(ks[0], (B, T, E), jnp.float32)
        w_lqkv, b_lqkv = lin(ks[1], LD, 3 * LD)
        w_gqkv, b_gqkv = lin(ks[2], LD, 3 * LD)
        w_comp, b_comp = lin(ks[3], R * E, E)
        w_lproj, b_lproj = lin(ks[4], LD, LD)
        w_gproj, b_gproj = lin(ks[5], LD, LD)
        w_gate, b_gate = lin(ks[6], E, 2)
        return {'x': x, 'w_lqkv': w_lqkv, 'b_lqkv': b_lqkv, 'w_gqkv': w_gqkv, 'b_gqkv': b_gqkv, 'w_comp': w_comp, 'b_comp': b_comp, 'w_lproj': w_lproj, 'b_lproj': b_lproj, 'w_gproj': w_gproj, 'b_gproj': b_gproj, 'w_gate': w_gate, 'b_gate': b_gate}
    _L1_attn_in = _L1_attn_setup()

    def _L1_ffn_setup():
        import jax, jax.numpy as jnp
        import numpy as np
        EMBED = 128
        D_FF = 4 * EMBED
        N_EXPERTS = 8
        TOP_K = 2
        B, S = (2, 128)
        key = jax.random.key(seed)
        ks = jax.random.split(key, 10)
        sc_d = 1.0 / np.sqrt(EMBED)
        sc_h = 1.0 / np.sqrt(D_FF)
        return {'inputs': jax.random.normal(ks[0], (B, S, EMBED), jnp.float32), 'rw1': jax.random.normal(ks[1], (EMBED, D_FF), jnp.float32) * sc_d, 'rb1': jnp.zeros((D_FF,), jnp.float32), 'rw2': jax.random.normal(ks[2], (D_FF, N_EXPERTS), jnp.float32) * sc_h, 'rb2': jnp.zeros((N_EXPERTS,), jnp.float32), 'W1': jax.random.normal(ks[3], (N_EXPERTS, EMBED, D_FF), jnp.float32) * sc_d, 'b1': jnp.zeros((N_EXPERTS, D_FF), jnp.float32), 'W2': jax.random.normal(ks[4], (N_EXPERTS, D_FF, EMBED), jnp.float32) * sc_h, 'b2': jnp.zeros((N_EXPERTS, EMBED), jnp.float32)}
    _L1_ffn_in = _L1_ffn_setup()

    def _L2_attn_setup():
        import jax, jax.numpy as jnp
        import numpy as np
        DIM = 128
        B, N = (8, 512)
        EPS = 1e-06
        key = jax.random.key(seed)
        k1, k2, k3, k4 = jax.random.split(key, 4)
        x = jax.random.normal(k1, (B, N, DIM), dtype=jnp.float32)
        s = 1.0 / np.sqrt(DIM)
        W_qkv = jax.random.uniform(k2, (3 * DIM, DIM), jnp.float32, -s, s)
        W_out = jax.random.uniform(k3, (DIM, DIM), jnp.float32, -s, s)
        b_out = jax.random.uniform(k4, (DIM,), jnp.float32, -s, s)
        return {'x': x, 'W_qkv': W_qkv, 'W_out': W_out, 'b_out': b_out}
    _L2_attn_in = _L2_attn_setup()

    def _L2_ffn_setup():
        import jax, jax.numpy as jnp
        import numpy as np
        DIM = 128
        HID = 64
        N_EXPERTS = 16
        TOP_K = 4
        key = jax.random.key(seed)
        ks = jax.random.split(key, 8)
        s = 0.02
        x = jax.random.normal(ks[0], (2, 128, DIM), dtype=jnp.float32)
        gate_w = jax.random.normal(ks[1], (N_EXPERTS, DIM), dtype=jnp.float32) * s
        w1 = jax.random.normal(ks[2], (N_EXPERTS, HID, DIM), dtype=jnp.float32) * s
        w3 = jax.random.normal(ks[3], (N_EXPERTS, HID, DIM), dtype=jnp.float32) * s
        w2 = jax.random.normal(ks[4], (N_EXPERTS, DIM, HID), dtype=jnp.float32) * s
        sw1 = jax.random.normal(ks[5], (HID, DIM), dtype=jnp.float32) * s
        sw3 = jax.random.normal(ks[6], (HID, DIM), dtype=jnp.float32) * s
        sw2 = jax.random.normal(ks[7], (DIM, HID), dtype=jnp.float32) * s
        return {'x': x, 'gate_w': gate_w, 'w1': w1, 'w3': w3, 'w2': w2, 'sw1': sw1, 'sw3': sw3, 'sw2': sw2}
    _L2_ffn_in = _L2_ffn_setup()

    def _L3_attn_setup():
        import jax, jax.numpy as jnp
        import numpy as np
        import math
        B, T, D, H = (4, 256, 128, 16)
        HD = D // H
        key = jax.random.key(seed)
        ks = jax.random.split(key, 10)
        s = 0.02
        return {'hidden_states': jax.random.normal(ks[0], (B, T, D), jnp.float32), 'Wq': jax.random.normal(ks[1], (H, D, HD), jnp.float32) * s, 'bq': jnp.zeros((H, HD), jnp.float32), 'Wk': jax.random.normal(ks[2], (H, D, HD), jnp.float32) * s, 'bk': jnp.zeros((H, HD), jnp.float32), 'Wv': jax.random.normal(ks[3], (H, D, HD), jnp.float32) * s, 'bv': jnp.zeros((H, HD), jnp.float32), 'Wo': jax.random.normal(ks[4], (H, HD, D), jnp.float32) * s, 'bo': jnp.zeros((H, D), jnp.float32), 'gate': jnp.ones((H,), jnp.float32)}
    _L3_attn_in = _L3_attn_setup()

    def _L3_ffn_setup():
        import jax, jax.numpy as jnp
        import numpy as np
        B, S, H = (2, 256, 128)
        E, F, K = (64, 64, 8)
        G, TG = (8, 4)
        SCALE = 2.5
        F_SH = 64

        def _gate(x, gate_w, gate_bias):
            scores = jax.nn.sigmoid(x @ gate_w.T)
            sc = scores + gate_bias[None, :]
            T = x.shape[0]
            group_scores = jax.lax.top_k(sc.reshape(T, G, E // G), 2)[0].sum(-1)
            _, gidx = jax.lax.top_k(group_scores, TG)
            gmask = jnp.zeros((T, G), sc.dtype).at[jnp.arange(T)[:, None], gidx].set(1.0)
            smask = jnp.repeat(gmask, E // G, axis=1)
            masked = jnp.where(smask > 0, sc, -jnp.inf)
            _, tidx = jax.lax.top_k(masked, K)
            tw = jnp.take_along_axis(scores, tidx, axis=1)
            tw = tw / (tw.sum(-1, keepdims=True) + 1e-20)
            return (tidx, tw * SCALE)
        key = jax.random.key(seed)
        ks = jax.random.split(key, 9)

        def w(k, shape, fan_in):
            return jax.random.normal(k, shape, jnp.float32) / np.float32(np.sqrt(fan_in))
        return {'hidden_states': jax.random.normal(ks[0], (B, S, H), jnp.float32), 'gate_w': w(ks[1], (E, H), H), 'gate_bias': jax.random.normal(ks[2], (E,), jnp.float32) * 0.01, 'We_gate': w(ks[3], (E, H, F), H), 'We_up': w(ks[4], (E, H, F), H), 'We_down': w(ks[5], (E, F, H), F), 'Ws_gate': w(ks[6], (H, F_SH), H), 'Ws_up': w(ks[7], (H, F_SH), H), 'Ws_down': w(ks[8], (F_SH, H), F_SH)}
    _L3_ffn_in = _L3_ffn_setup()
    _d = {'L0_attn_x': _L0_attn_in['x'], 'L0_attn_w_disp': _L0_attn_in['w_disp'], 'L0_attn_b_disp': _L0_attn_in['b_disp'], 'L0_attn_w_val': _L0_attn_in['w_val'], 'L0_attn_b_val': _L0_attn_in['b_val'], 'L0_attn_rel_pos_emb': _L0_attn_in['rel_pos_emb'], 'L0_attn_w_state': _L0_attn_in['w_state'], 'L0_attn_b_state': _L0_attn_in['b_state'], 'L0_attn_w_strain': _L0_attn_in['w_strain'], 'L0_attn_b_strain': _L0_attn_in['b_strain'], 'L0_attn_w_state_i': _L0_attn_in['w_state_i'], 'L0_attn_w_state_j': _L0_attn_in['w_state_j'], 'L0_attn_w_pos': _L0_attn_in['w_pos'], 'L0_attn_w_bond_out': _L0_attn_in['w_bond_out'], 'L0_attn_b_bond_out': _L0_attn_in['b_bond_out'], 'L0_attn_w_damage': _L0_attn_in['w_damage'], 'L0_attn_b_damage': _L0_attn_in['b_damage'], 'L0_attn_w_damage_out': _L0_attn_in['w_damage_out'], 'L0_attn_b_damage_out': _L0_attn_in['b_damage_out'], 'L0_attn_w_cproj': _L0_attn_in['w_cproj'], 'L0_attn_b_cproj': _L0_attn_in['b_cproj'], 'L0_ffn_router_w': _L0_ffn_in['router_w'], 'L0_ffn_lora_down': _L0_ffn_in['lora_down'], 'L0_ffn_lora_up': _L0_ffn_in['lora_up'], 'L1_attn_w_lqkv': _L1_attn_in['w_lqkv'], 'L1_attn_b_lqkv': _L1_attn_in['b_lqkv'], 'L1_attn_w_gqkv': _L1_attn_in['w_gqkv'], 'L1_attn_b_gqkv': _L1_attn_in['b_gqkv'], 'L1_attn_w_comp': _L1_attn_in['w_comp'], 'L1_attn_b_comp': _L1_attn_in['b_comp'], 'L1_attn_w_lproj': _L1_attn_in['w_lproj'], 'L1_attn_b_lproj': _L1_attn_in['b_lproj'], 'L1_attn_w_gproj': _L1_attn_in['w_gproj'], 'L1_attn_b_gproj': _L1_attn_in['b_gproj'], 'L1_attn_w_gate': _L1_attn_in['w_gate'], 'L1_attn_b_gate': _L1_attn_in['b_gate'], 'L1_ffn_rw1': _L1_ffn_in['rw1'], 'L1_ffn_rb1': _L1_ffn_in['rb1'], 'L1_ffn_rw2': _L1_ffn_in['rw2'], 'L1_ffn_rb2': _L1_ffn_in['rb2'], 'L1_ffn_W1': _L1_ffn_in['W1'], 'L1_ffn_b1': _L1_ffn_in['b1'], 'L1_ffn_W2': _L1_ffn_in['W2'], 'L1_ffn_b2': _L1_ffn_in['b2'], 'L2_attn_W_qkv': _L2_attn_in['W_qkv'], 'L2_attn_W_out': _L2_attn_in['W_out'], 'L2_attn_b_out': _L2_attn_in['b_out'], 'L2_ffn_gate_w': _L2_ffn_in['gate_w'], 'L2_ffn_w1': _L2_ffn_in['w1'], 'L2_ffn_w3': _L2_ffn_in['w3'], 'L2_ffn_w2': _L2_ffn_in['w2'], 'L2_ffn_sw1': _L2_ffn_in['sw1'], 'L2_ffn_sw3': _L2_ffn_in['sw3'], 'L2_ffn_sw2': _L2_ffn_in['sw2'], 'L3_attn_Wq': _L3_attn_in['Wq'], 'L3_attn_bq': _L3_attn_in['bq'], 'L3_attn_Wk': _L3_attn_in['Wk'], 'L3_attn_bk': _L3_attn_in['bk'], 'L3_attn_Wv': _L3_attn_in['Wv'], 'L3_attn_bv': _L3_attn_in['bv'], 'L3_attn_Wo': _L3_attn_in['Wo'], 'L3_attn_bo': _L3_attn_in['bo'], 'L3_attn_gate': _L3_attn_in['gate'], 'L3_ffn_gate_w': _L3_ffn_in['gate_w'], 'L3_ffn_gate_bias': _L3_ffn_in['gate_bias'], 'L3_ffn_We_gate': _L3_ffn_in['We_gate'], 'L3_ffn_We_up': _L3_ffn_in['We_up'], 'L3_ffn_We_down': _L3_ffn_in['We_down'], 'L3_ffn_Ws_gate': _L3_ffn_in['Ws_gate'], 'L3_ffn_Ws_up': _L3_ffn_in['Ws_up'], 'L3_ffn_Ws_down': _L3_ffn_in['Ws_down']}
    _x0 = _d['L0_attn_x']
    _d['L0_attn_x'] = jax.random.normal(jax.random.fold_in(jax.random.key(seed), 1), (8, 512, 128), dtype=_x0.dtype)
    del _x0
    return _d

def reference(L0_attn_x, L0_attn_w_disp, L0_attn_b_disp, L0_attn_w_val, L0_attn_b_val, L0_attn_rel_pos_emb, L0_attn_w_state, L0_attn_b_state, L0_attn_w_strain, L0_attn_b_strain, L0_attn_w_state_i, L0_attn_w_state_j, L0_attn_w_pos, L0_attn_w_bond_out, L0_attn_b_bond_out, L0_attn_w_damage, L0_attn_b_damage, L0_attn_w_damage_out, L0_attn_b_damage_out, L0_attn_w_cproj, L0_attn_b_cproj, L0_ffn_router_w, L0_ffn_lora_down, L0_ffn_lora_up, L1_attn_w_lqkv, L1_attn_b_lqkv, L1_attn_w_gqkv, L1_attn_b_gqkv, L1_attn_w_comp, L1_attn_b_comp, L1_attn_w_lproj, L1_attn_b_lproj, L1_attn_w_gproj, L1_attn_b_gproj, L1_attn_w_gate, L1_attn_b_gate, L1_ffn_rw1, L1_ffn_rb1, L1_ffn_rw2, L1_ffn_rb2, L1_ffn_W1, L1_ffn_b1, L1_ffn_W2, L1_ffn_b2, L2_attn_W_qkv, L2_attn_W_out, L2_attn_b_out, L2_ffn_gate_w, L2_ffn_w1, L2_ffn_w3, L2_ffn_w2, L2_ffn_sw1, L2_ffn_sw3, L2_ffn_sw2, L3_attn_Wq, L3_attn_bq, L3_attn_Wk, L3_attn_bk, L3_attn_Wv, L3_attn_bv, L3_attn_Wo, L3_attn_bo, L3_attn_gate, L3_ffn_gate_w, L3_ffn_gate_bias, L3_ffn_We_gate, L3_ffn_We_up, L3_ffn_We_down, L3_ffn_Ws_gate, L3_ffn_Ws_up, L3_ffn_Ws_down):

    def _L0_attn_ref(x, w_disp, b_disp, w_val, b_val, rel_pos_emb, w_state, b_state, w_strain, b_strain, w_state_i, w_state_j, w_pos, w_bond_out, b_bond_out, w_damage, b_damage, w_damage_out, b_damage_out, w_cproj, b_cproj):
        import jax, jax.numpy as jnp
        import numpy as np
        B, T, C = (2, 256, 128)
        NH = 16
        HS = C // NH
        BD = max(HS // 4, 16)
        HORIZON = 32

        def _windows(t, delta):
            padded = jnp.pad(t, ((0, 0), (0, 0), (delta - 1, 0), (0, 0)))
            idx = jnp.arange(t.shape[2])[:, None] + jnp.arange(delta)[None, :]
            return padded[:, :, idx]
        Bx, Tx, Cx = x.shape
        delta = min(HORIZON, Tx)
        gelu = lambda v: jax.nn.gelu(v, approximate=False)
        disp = (x @ w_disp + b_disp).reshape(Bx, Tx, NH, BD).transpose(0, 2, 1, 3)
        val = (x @ w_val + b_val).reshape(Bx, Tx, NH, HS).transpose(0, 2, 1, 3)
        disp_win = _windows(disp, delta)
        val_win = _windows(val, delta)
        cmask = jnp.arange(Tx)[:, None] - delta + 1 + jnp.arange(delta)[None, :] >= 0
        cmask_f = cmask.astype(x.dtype)
        strain = disp_win - disp[:, :, :, None, :]
        strain_for_state = strain @ w_state + b_state
        valid_counts = jnp.clip(cmask_f.sum(axis=-1), 1.0)
        state = (strain_for_state * cmask_f[None, None, :, :, None]).sum(axis=3) / valid_counts[None, None, :, None]
        state_win = _windows(state, delta)
        rel_emb = rel_pos_emb[:delta]
        bond_act = gelu(strain @ w_strain + b_strain + state[:, :, :, None, :] @ w_state_i + state_win @ w_state_j + rel_emb @ w_pos)
        bond_logits = (bond_act @ w_bond_out)[..., 0] + b_bond_out[0]
        damage_act = gelu(strain @ w_damage + b_damage)
        damage = jax.nn.sigmoid((damage_act @ w_damage_out)[..., 0] + b_damage_out[0])
        logits = bond_logits - damage * 10.0
        logits = jnp.where(cmask[None, None], logits, -jnp.inf)
        weights = jax.nn.softmax(logits, axis=-1)
        out = jnp.einsum('bntd,bntde->bnte', weights, val_win)
        out = out.transpose(0, 2, 1, 3).reshape(Bx, Tx, Cx)
        return out @ w_cproj + b_cproj

    def _L0_ffn_ref(x, router_w, lora_down, lora_up):
        import jax, jax.numpy as jnp
        import numpy as np
        B, L, H = (32, 64, 128)
        E, R, TOP_K = (8, 16, 2)

        def _gates(cls, router_w):
            logits = jnp.einsum('bh,eh->be', cls, router_w)
            top_vals, top_idx = jax.lax.top_k(logits, TOP_K)
            mask = jnp.full_like(logits, -jnp.inf)
            rows = jnp.arange(logits.shape[0])[:, None]
            mask = mask.at[rows, top_idx].set(top_vals)
            return jax.nn.softmax(mask, axis=1)
        gates = _gates(x[:, 0, :], router_w)
        down = jnp.einsum('blh,erh->bler', x, lora_down)
        weighted = jnp.einsum('bler,ehr,be->blh', down, lora_up, gates)
        return x + weighted

    def _L1_attn_ref(x, w_lqkv, b_lqkv, w_gqkv, b_gqkv, w_comp, b_comp, w_lproj, b_lproj, w_gproj, b_gproj, w_gate, b_gate):
        import jax, jax.numpy as jnp
        import numpy as np
        B, T, E = (2, 512, 128)
        N_HEAD = 16
        HEAD_DIM = E // N_HEAD
        R = 4
        LD = E // 2
        HH = N_HEAD // 2

        def _split_heads(t, L):
            return t.reshape(t.shape[0], L, HH, HEAD_DIM).transpose(0, 2, 1, 3)

        def _causal_attn(q, k, v):
            L = q.shape[2]
            scores = jnp.einsum('bhqd,bhkd->bhqk', q, k) / jnp.sqrt(jnp.float32(HEAD_DIM))
            mask = jnp.tril(jnp.ones((L, L), dtype=bool))
            scores = jnp.where(mask, scores, -jnp.inf)
            att = jax.nn.softmax(scores, axis=-1)
            return jnp.einsum('bhqk,bhkd->bhqd', att, v)
        Bx, Tx, C = x.shape
        local_x = x[..., :LD]
        lq, lk, lv = jnp.split(local_x @ w_lqkv + b_lqkv, 3, axis=-1)
        local_out = _causal_attn(_split_heads(lq, Tx), _split_heads(lk, Tx), _split_heads(lv, Tx))
        local_out = local_out.transpose(0, 2, 1, 3).reshape(Bx, Tx, LD)
        local_out = local_out @ w_lproj + b_lproj
        Tc = Tx // R
        compressed = x.reshape(Bx, Tc, R * C) @ w_comp + b_comp
        cg = compressed[..., LD:]
        gq, gk, gv = jnp.split(cg @ w_gqkv + b_gqkv, 3, axis=-1)
        global_out = _causal_attn(_split_heads(gq, Tc), _split_heads(gk, Tc), _split_heads(gv, Tc))
        global_out = global_out.transpose(0, 2, 1, 3).reshape(Bx, Tc, LD)
        global_out = global_out @ w_gproj + b_gproj
        global_out = jnp.repeat(global_out, R, axis=1)[:, :Tx, :]
        combined = jnp.concatenate([local_out, global_out], axis=-1)
        gate_w = jax.nn.softmax(combined @ w_gate + b_gate, axis=-1)
        return jnp.concatenate([gate_w[..., 0:1] * local_out, gate_w[..., 1:2] * global_out], axis=-1)

    def _L1_ffn_ref(inputs, rw1, rb1, rw2, rb2, W1, b1, W2, b2):
        import jax, jax.numpy as jnp
        import numpy as np
        EMBED = 128
        D_FF = 4 * EMBED
        N_EXPERTS = 8
        TOP_K = 2
        B, S = (2, 128)
        Bb, Ss, D = inputs.shape
        T = Bb * Ss
        xf = inputs.reshape(T, D)
        score = jax.nn.relu(xf @ rw1 + rb1) @ rw2 + rb2
        _, topi = jax.lax.top_k(score, TOP_K)
        mask = jnp.zeros(score.shape, bool).at[jnp.arange(T)[:, None], topi].set(True)
        gate = jax.nn.softmax(jnp.where(mask, score, -jnp.inf), axis=-1)
        out = jnp.zeros_like(xf)
        for e in range(N_EXPERTS):
            h = jax.nn.relu(xf @ W1[e] + b1[e])
            y = h @ W2[e] + b2[e]
            out = out + gate[:, e:e + 1] * y
        return out.reshape(Bb, Ss, D)

    def _L2_attn_ref(x, W_qkv, W_out, b_out):
        import jax, jax.numpy as jnp
        import numpy as np
        DIM = 128
        B, N = (8, 512)
        EPS = 1e-06
        qkv = jnp.einsum('bnd,ed->bne', x, W_qkv)
        q, k, v = jnp.split(qkv, 3, axis=-1)
        q = jax.nn.relu(q) + EPS
        k = jax.nn.relu(k) + EPS
        kv = jnp.einsum('bnd,bne->bde', k, v)
        z = 1.0 / (jnp.einsum('bnd,bd->bn', q, k.sum(axis=1)) + EPS)
        attn = jnp.einsum('bnd,bde,bn->bne', q, kv, z)
        return jnp.einsum('bne,fe->bnf', attn, W_out) + b_out

    def _L2_ffn_ref(x, gate_w, w1, w3, w2, sw1, sw3, sw2):
        import jax, jax.numpy as jnp
        import numpy as np
        DIM = 128
        HID = 64
        N_EXPERTS = 16
        TOP_K = 4
        bsz, seq_len, dim = x.shape
        xf = x.reshape(-1, dim)
        T = xf.shape[0]
        probs = jax.nn.softmax(xf @ gate_w.T, axis=-1)
        top_w, top_idx = jax.lax.top_k(probs, TOP_K)
        top_w = top_w / jnp.sum(top_w, axis=-1, keepdims=True)
        rows = jnp.arange(T)[:, None]
        combine = jnp.zeros((T, N_EXPERTS), dtype=xf.dtype).at[rows, top_idx].set(top_w)
        h1 = jnp.einsum('td,ehd->teh', xf, w1)
        h3 = jnp.einsum('td,ehd->teh', xf, w3)
        act = jax.nn.silu(h1) * h3
        eout = jnp.einsum('teh,edh->ted', act, w2)
        moe_out = jnp.einsum('ted,te->td', eout, combine)
        shared = jax.nn.silu(xf @ sw1.T) * (xf @ sw3.T) @ sw2.T
        return (moe_out + shared).reshape(bsz, seq_len, dim)

    def _L3_attn_ref(hidden_states, Wq, bq, Wk, bk, Wv, bv, Wo, bo, gate):
        import jax, jax.numpy as jnp
        import numpy as np
        import math
        B, T, D, H = (4, 256, 128, 16)
        HD = D // H
        scale = 1.0 / math.sqrt(HD)
        q = jnp.einsum('btd,hdk->bhtk', hidden_states, Wq) + bq[None, :, None, :]
        k = jnp.einsum('btd,hdk->bhtk', hidden_states, Wk) + bk[None, :, None, :]
        v = jnp.einsum('btd,hdk->bhtk', hidden_states, Wv) + bv[None, :, None, :]
        scores = jnp.einsum('bhtk,bhsk->bhts', q, k) * scale
        weights = jax.nn.softmax(scores, axis=-1)
        out = jnp.einsum('bhts,bhsk->bhtk', weights, v)
        norms = jnp.linalg.norm(out, axis=-1)
        denom = jnp.maximum(norms.mean(axis=(0, 2)), 1e-05)
        out_norm = out / denom[None, :, None, None]
        gate_val = jnp.clip(gate, 0.0, 1.0)
        proj = (jnp.einsum('bhtk,hkd->bhtd', out_norm, Wo) + bo[None, :, None, :]) * gate_val[None, :, None, None]
        return proj.sum(axis=1) / H

    def _L3_ffn_ref(hidden_states, gate_w, gate_bias, We_gate, We_up, We_down, Ws_gate, Ws_up, Ws_down):
        import jax, jax.numpy as jnp
        import numpy as np
        B, S, H = (2, 256, 128)
        E, F, K = (64, 64, 8)
        G, TG = (8, 4)
        SCALE = 2.5
        F_SH = 64

        def _gate(x, gate_w, gate_bias):
            scores = jax.nn.sigmoid(x @ gate_w.T)
            sc = scores + gate_bias[None, :]
            T = x.shape[0]
            group_scores = jax.lax.top_k(sc.reshape(T, G, E // G), 2)[0].sum(-1)
            _, gidx = jax.lax.top_k(group_scores, TG)
            gmask = jnp.zeros((T, G), sc.dtype).at[jnp.arange(T)[:, None], gidx].set(1.0)
            smask = jnp.repeat(gmask, E // G, axis=1)
            masked = jnp.where(smask > 0, sc, -jnp.inf)
            _, tidx = jax.lax.top_k(masked, K)
            tw = jnp.take_along_axis(scores, tidx, axis=1)
            tw = tw / (tw.sum(-1, keepdims=True) + 1e-20)
            return (tidx, tw * SCALE)
        b, s, h = hidden_states.shape
        x = hidden_states.reshape(-1, h).astype(jnp.float32)
        tidx, tw = _gate(x, gate_w, gate_bias)
        T = x.shape[0]
        w_dense = jnp.zeros((T, E), tw.dtype).at[jnp.arange(T)[:, None], tidx].add(tw)

        def body(acc, ws):
            wg, wu, wdn, cw = ws
            hmid = jax.nn.silu(x @ wg) * (x @ wu)
            return (acc + cw[:, None] * (hmid @ wdn), None)
        y, _ = jax.lax.scan(body, jnp.zeros_like(x), (We_gate, We_up, We_down, w_dense.T))
        y = y.reshape(b, s, h)
        shared = jax.nn.silu(hidden_states @ Ws_gate) * (hidden_states @ Ws_up) @ Ws_down
        return y + shared
    x = L0_attn_x
    xn = _layernorm(x, axis=-1)
    s = _L0_attn_ref(xn, L0_attn_w_disp, L0_attn_b_disp, L0_attn_w_val, L0_attn_b_val, L0_attn_rel_pos_emb, L0_attn_w_state, L0_attn_b_state, L0_attn_w_strain, L0_attn_b_strain, L0_attn_w_state_i, L0_attn_w_state_j, L0_attn_w_pos, L0_attn_w_bond_out, L0_attn_b_bond_out, L0_attn_w_damage, L0_attn_b_damage, L0_attn_w_damage_out, L0_attn_b_damage_out, L0_attn_w_cproj, L0_attn_b_cproj)
    g = _silu(_L0_ffn_ref(xn, L0_ffn_router_w, L0_ffn_lora_down, L0_ffn_lora_up))
    x = x + s * g
    xn = _layernorm(x, axis=-1)
    s = _L1_attn_ref(xn, L1_attn_w_lqkv, L1_attn_b_lqkv, L1_attn_w_gqkv, L1_attn_b_gqkv, L1_attn_w_comp, L1_attn_b_comp, L1_attn_w_lproj, L1_attn_b_lproj, L1_attn_w_gproj, L1_attn_b_gproj, L1_attn_w_gate, L1_attn_b_gate)
    g = _silu(_L1_ffn_ref(xn, L1_ffn_rw1, L1_ffn_rb1, L1_ffn_rw2, L1_ffn_rb2, L1_ffn_W1, L1_ffn_b1, L1_ffn_W2, L1_ffn_b2))
    x = x + s * g
    xn = _layernorm(x, axis=-1)
    s = _L2_attn_ref(xn, L2_attn_W_qkv, L2_attn_W_out, L2_attn_b_out)
    g = _silu(_L2_ffn_ref(xn, L2_ffn_gate_w, L2_ffn_w1, L2_ffn_w3, L2_ffn_w2, L2_ffn_sw1, L2_ffn_sw3, L2_ffn_sw2))
    x = x + s * g
    xn = _layernorm(x, axis=-1)
    s = _L3_attn_ref(xn, L3_attn_Wq, L3_attn_bq, L3_attn_Wk, L3_attn_bk, L3_attn_Wv, L3_attn_bv, L3_attn_Wo, L3_attn_bo, L3_attn_gate)
    g = _silu(_L3_ffn_ref(xn, L3_ffn_gate_w, L3_ffn_gate_bias, L3_ffn_We_gate, L3_ffn_We_up, L3_ffn_We_down, L3_ffn_Ws_gate, L3_ffn_Ws_up, L3_ffn_Ws_down))
    x = x + s * g
    return x

_drawn_inputs = setup_inputs


def setup_inputs(seed=0):
    import zlib

    import numpy as np

    out = dict(_drawn_inputs(seed))
    spreads = {'L0_attn_b_disp': (0.0, 0.8),
     'L0_attn_b_val': (0.0, 0.428),
     'L0_attn_b_state': (0.0, 0.8),
     'L0_attn_b_strain': (0.0, 0.8),
     'L0_attn_b_damage': (0.0, 0.8),
     'L0_attn_b_cproj': (0.0, 0.1),
     'L1_ffn_rb1': (0.0, 0.8),
     'L1_ffn_rb2': (0.0, 0.8),
     'L1_ffn_b1': (0.0, 0.8),
     'L1_ffn_b2': (0.0, 0.8),
     'L3_attn_bq': (0.0, 0.8),
     'L3_attn_bk': (0.0, 0.8),
     'L3_attn_bv': (0.0, 0.8),
     'L3_attn_bo': (0.0, 0.8),
     'L3_attn_gate': (1.0, 0.6)}
    factors = {'L0_attn_w_disp': 8.0,
     'L0_attn_w_val': 7.569,
     'L0_attn_rel_pos_emb': 8.0,
     'L0_attn_w_state': 8.0,
     'L0_attn_w_strain': 8.0,
     'L0_attn_w_state_i': 8.0,
     'L0_attn_w_state_j': 8.0,
     'L0_attn_w_pos': 8.0,
     'L0_attn_w_bond_out': 8.0,
     'L0_attn_w_damage': 8.0,
     'L0_attn_w_damage_out': 8.0,
     'L0_attn_w_cproj': 2.953,
     'L1_attn_w_lqkv': 8.0,
     'L1_attn_b_lqkv': 8.0,
     'L1_attn_w_gqkv': 8.0,
     'L1_attn_b_gqkv': 8.0,
     'L1_attn_w_comp': 8.0,
     'L1_attn_b_comp': 8.0,
     'L1_attn_w_lproj': 8.0,
     'L1_attn_b_lproj': 8.0,
     'L1_attn_w_gproj': 8.0,
     'L1_attn_b_gproj': 8.0,
     'L1_attn_w_gate': 8.0,
     'L1_attn_b_gate': 8.0,
     'L1_ffn_rw1': 8.0,
     'L1_ffn_rw2': 8.0,
     'L1_ffn_W1': 8.0,
     'L1_ffn_W2': 8.0,
     'L2_attn_W_qkv': 8.0,
     'L2_attn_W_out': 8.0,
     'L2_attn_b_out': 8.0,
     'L2_ffn_gate_w': 8.0,
     'L2_ffn_w1': 8.0,
     'L2_ffn_w3': 8.0,
     'L2_ffn_w2': 8.0,
     'L2_ffn_sw1': 8.0,
     'L2_ffn_sw3': 8.0,
     'L2_ffn_sw2': 8.0,
     'L3_attn_Wq': 8.0,
     'L3_attn_Wk': 8.0,
     'L3_attn_Wv': 8.0,
     'L3_attn_Wo': 8.0,
     'L3_ffn_gate_w': 8.0,
     'L3_ffn_gate_bias': 8.0,
     'L3_ffn_We_gate': 8.0,
     'L3_ffn_We_up': 8.0,
     'L3_ffn_We_down': 8.0,
     'L3_ffn_Ws_gate': 8.0,
     'L3_ffn_Ws_up': 8.0,
     'L3_ffn_Ws_down': 8.0}
    for name, (base, spread) in spreads.items():
        noise = np.random.default_rng([zlib.crc32(name.encode()), seed]).standard_normal(out[name].shape)
        drawn = base * np.exp(spread * noise) if base else spread * noise
        out[name] = jnp.asarray(drawn.astype(out[name].dtype))
    for name, factor in factors.items():
        out[name] = (out[name] * factor).astype(out[name].dtype)
    return out
```

```python
from contextlib import ExitStack

import numpy as np
import concourse.bass as bass
from concourse import mybir

B, T, C = 8, 512, 128
P = 128
NT = T // P
NH, HD, BD, HOR = 16, 8, 16, 32
FF, E1 = 512, 8
NF = FF // P
E2, K2 = 16, 4
E3, G3, TG3, K3 = 64, 8, 4, 8
R1 = 4
LN_EPS = 1e-5
LD = C // 2
NEG, GONE = -1e30, -3e38
HI3 = 2.5
BAND = P + HOR
PAD = HOR
TERMS = 9 * HD
RING = 5
WSLOTS = 5

FP32 = mybir.dt.float32
BF16 = mybir.dt.bfloat16
ALU = mybir.AluOpType
ACT = mybir.ActivationFunctionType
AX = mybir.AxisListType


def shape_constants():
    p = np.arange(P)
    col = lambda n: np.arange(n)[None]
    c = {}
    c["ident"] = np.eye(P)
    c["sel_head0"] = (p[:, None] == col(P) % 8)
    c["sel_head1"] = (p[:, None] == 8 + col(P) % 8)
    c["sel_den"] = (p[:, None] == 16 * (col(P) // 16) + 8)
    c["sum_group"] = (p[:, None] // 16 == col(8)) & (p[:, None] % 16 < 8)
    c["block16"] = (p[:, None] // 16 == col(8))
    c["slot_mask"] = np.concatenate([(col(32) == 8 * q + p[:, None] // 16) for q in range(4)], 1)
    c["edge"] = np.concatenate([np.where(col(HOR) < 16 * u + p[:, None] // 8, NEG, 0)
                                for u in range(2) for _ in range(2)], 1)
    c["count_fix"] = np.tile(HOR / (col(HOR) + 1.0), (P, 1))
    c["causal_qk"] = np.where(col(P) > p[:, None], NEG, 0)
    c["causal_kq"] = np.where(p[:, None] > col(P), NEG, 0)
    c["pad_sel0"] = (16 * (p[:, None] % 64 // 8) + p[:, None] % 8 == col(P)) & (p[:, None] < 64)
    c["pad_sel1"] = (16 * (p[:, None] % 64 // 8) + p[:, None] % 8 == col(P)) & (p[:, None] >= 64)
    c["rep16"] = (p[:, None] == col(P) % 16)
    c["head_row0"] = (p[:, None] == col(P) // 16)
    c["head_row1"] = (p[:, None] == 8 + col(P) // 16)
    c["expand4"] = (p[:, None] == col(T) // R1)
    c["hot64"] = (p[:, None] % 64 == col(64))
    c["hot16"] = (p[:, None] % 16 == col(16))
    at, where = 0, {}
    for k, v in c.items():
        where[k] = (at, at + v.shape[1])
        at += v.shape[1]
    return np.concatenate([np.asarray(v, np.float32) for v in c.values()], 1), where


PER = {
    "acc1": 7, "act": 32, "act_used": 32, "av": 42, "band0": 16, "band1": 16, "band2": 16, "band3": 16,
    "band_used": 4, "best_dif": 3, "best_exp": 3, "by_key": 4, "cb": 2, "cg_ps": 1, "cgt": 1, "ct": 2, "ct_ps": 2,
    "dam": 2, "dam_ps": 2, "damage": 1, "den": 3, "den3": 2, "disp": 2, "disp_ps": 2, "down": 42, "dve": 138,
    "e_stored": 16, "exp_t": 4, "f": 4, "f0_ps": 4, "f0_sb": 2, "f1_ps": 4, "g1": 1, "g1_row": 1, "g_saved": 16,
    "gate": 4, "go": 1, "go_all": 1, "go_seen": 1, "h1": 32, "h1_ps": 32, "k_ones": 48, "k_out": 160, "l2_ps": 5,
    "l2_sb": 4, "lexp": 1, "lmax": 4, "lmax_b": 2, "lmax_row": 1, "lmax_t": 1, "lo": 1, "logit": 1, "logit_out": 8,
    "logit_t": 4, "max": 72, "mix_dif": 1, "mix_tanh": 1, "n3_ps": 1, "n_saved": 32, "nm": 3, "nm_in": 144,
    "nm_t": 3, "nmt": 3, "o2": 1, "o_saved": 16, "on": 4, "os": 4, "p": 52, "p_ps": 2, "p_sb": 2, "pre_dve": 24,
    "pre_pool": 8, "proj": 3, "pv": 26, "q_out": 96, "q_ps": 2, "q_zero": 16, "qe": 1, "qk": 6, "qk_ps": 6, "r": 4,
    "r_ps": 4, "rc3": 2, "rstd": 4, "s0": 1, "s1": 72, "s2": 52, "s3": 1, "sc1": 1, "sc_ps": 2, "shifted": 1,
    "sig3": 1, "skewed": 64, "sl": 42, "split": 3, "split_out_g": 128, "sq3": 1, "stack_zero": 4, "stacked": 192,
    "stacked_g": 96, "state": 2, "state_ps": 2, "u_ps": 42, "v": 3, "v_ps": 3, "val": 1, "val_ps": 1, "var": 4,
    "w1_in0": 64, "w1_in1": 64, "w1_in2": 64, "w1_in3": 32, "w1_in4": 32, "w1_used": 8, "w_ps": 42, "wmean": 1,
    "wsum": 7, "x": 3, "x_in": 16, "x_saved": 16, "xn": 4, "xt": 4, "xt_ps": 4, "z_stored0": 16, "z_stored1": 16,
    "z_stored2": 16, "z_stored3": 16,
}


PROLOGUE = ["w_consts", "w_nat", "w_small", "w_late", "scratch_zero", "nat_zero", "zero_ready", "pool_pro", "wt_ready",
            "wt_out", "pro_mm", "rd16", "act_pro", "dve_pro"]
FINAL = ["fin_w", "fin_n", "fin_sqrt", "fin_dve", "fin_fac", "fin_mm", "fin_w2", "fin_in0", "fin_in1", "fin_used0",
         "fin_used1", "fin_out0", "fin_out1", "fin_y", "fin_c"]


def at(name, b, n):
    return b * PER[name] + n


def s1_items(c):
    nt = c["n"] // P
    step = 1 if c["causal"] else 2
    return [(n, list(range(j, j + step))) for n in range(c["nh"]) for j in range(0, nt, step)]


def s2_items(c):
    return [(g, i, pr) for g in range(c["nh"] // 4) for i in range(c["n"] // P) for pr in range(2)]


ATTN = {"0": None, "L": dict(nh=8, n=T, causal=True), "G": dict(nh=8, n=P, causal=True), "A": dict(nh=16, n=T, causal=False)}


def tagged(name, tag, b, n):
    before = 0
    for t, c in ATTN.items():
        if t == tag:
            break
        if t == "G" and name in ("stacked", "q_out", "k_out"):
            continue
        if c is None:
            before += 1 if name in ("os", "den", "on", "proj") else 0
        else:
            before += {"qk_ps": 2, "qk": 2, "s1": len(s1_items(c)), "max": len(s1_items(c)), "s2": len(s2_items(c)),
                       "p": len(s2_items(c)), "pv": len(s2_items(c)) // 2, "stacked": 96,
                       "nm_in": 48, "on": 1, "q_out": 48, "k_out": 80}.get(name, 1)
    return at(name, b, before + n)


def paired(name, l, b, n):
    each = 1 if name in ("sc_ps", "cb", "ct_ps", "ct") else E2 // 2 + 1
    return at(name, b, n + (each if l == 3 else 0))


def build(nc, a, out):
    consts, where = shape_constants()
    NC = consts.shape[1]
    ctx = ExitStack()
    with ctx:
        def sb(name, shape, dt=FP32):
            return ctx.enter_context(nc.sbuf_tensor(name, shape, dt))

        S = {}
        for name in list(PER) + PROLOGUE + FINAL:
            S[name] = ctx.enter_context(nc.semaphore(name))

        def wait_alone(e, value):
            e.lower_val(value)
            e.wait_ge(S["nat_zero"], 1)

        stage_no = iter(range(1000))

        def stage_turn(e, b):
            r = e.alloc_register(f"turn{next(stage_no)}")
            e.reg_mov(r, b)
            v = e.snap(r)
            e.free_register(r)
            return v

        e_dram = nc.dram_tensor("e_scratch", (P, 4, T + HOR), FP32).ap()
        z_dram = nc.dram_tensor("band_scratch", (NT, NH, P, BAND), FP32).ap()
        q_dram = nc.dram_tensor("q_scratch", (NH, 3, HD, T), BF16).ap()
        k_dram = nc.dram_tensor("k_scratch", (NH, 5, HD, T), BF16).ap()
        qg_dram = nc.dram_tensor("qg_scratch", (NH // 2, 3, HD, T), BF16).ap()
        kg_dram = nc.dram_tensor("kg_scratch", (NH // 2, 5, HD, T), BF16).ap()
        x_dram = nc.dram_tensor("x_scratch", (B, P, NT, C), FP32).ap()
        g_dram = nc.dram_tensor("g_scratch", (B, P, NT, C), FP32).ap()
        o_dram = nc.dram_tensor("o_scratch", (B, P, 2, T), FP32).ap()
        n_dram = nc.dram_tensor("norm_scratch", (2, 8, B, T), FP32).ap()

        CN = sb("consts", [P, NC])
        cn = lambda k: CN[:, where[k][0]:where[k][1]]
        ident = cn("ident")
        identb = sb("identb", [P, P], BF16)
        maskb = sb("maskb", [P, 2, P], BF16)
        hot64b = sb("hot64b", [P, 64], BF16)
        hot16b = sb("hot16b", [48, 16], BF16)
        WT = sb("WT", [P, 36, P])
        T_GATES, T_LD, T_LU, T_QKV, T_WO2, T_W1, T_W3, T_W2, T_SW13, T_SW2, T_B = 0, 1, 2, 3, 6, 7, 15, 23, 31, 32, 33
        NTILE = 36
        W16 = sb("W16", [16, 144])
        REP = sb("REP", [P, 96])
        BDM = sb("BDM", [P, 6, 8, 16])
        WOUT = sb("WOUT", [P, 2, 4, 32])
        BVC = sb("BVC", [P, 5])
        RD = sb("RD", [P, HOR])
        RD16 = sb("RD16", [16, HOR])
        SC1 = sb("SC1", [P, 4])
        wdisp = sb("wdisp", [P, 256])
        wval = sb("wval", [P, C])
        WCPN = sb("WCPN", [P, C])
        WON = sb("WON", [P, C])
        WCP = sb("WCP", [P, 2, C])
        WOP = sb("WOP", [P, 2, C])
        WLG = sb("WLG", [LD, 2, LD])
        WLGP = sb("WLGP", [P, 2, LD])
        wqkv1 = sb("wqkv1", [LD, 2, 3 * LD])
        wcomp = sb("wcomp", [P, R1, LD])
        ROWS = sb("ROWS", [P, 128 + 128 + 64 + 64 + 256 + 2 + 128 + 128 + 64 + 64 + 64])
        rc = {}
        o_ = 0
        for k, n in (("b_val", 128), ("b_cproj", 128), ("b_lproj", 64), ("b_gproj", 64), ("w_gate", 256), ("b_gate", 2),
                     ("b_out", 128), ("bv", 128), ("gate_bias", 64), ("bvl", 64), ("bvg", 64)):
            rc[k] = ROWS[:, o_:o_ + n]
            o_ += n
        WDIF = sb("WDIF", [P, C + 1])
        COLS = sb("COLS", [P, 16])
        rw1 = sb("rw1", [P, FF])
        rw2 = sb("rw2", [P, NF, E1])
        rb2 = sb("rb2", [E1, 1])
        b2 = sb("b2", [E1, C])
        wqkv3 = sb("wqkv3", [P, 3, NH, HD])
        WG3 = sb("WG3", [P, E3, 64])
        WU3 = sb("WU3", [P, E3, 64])
        WD3 = sb("WD3", [P, E3 // 2, C])
        WS3 = sb("WS3", [P, 2, 64])
        WSD3 = sb("WSD3", [64, C])
        ONEZ = sb("ONEZ", [3, 2, P], BF16)
        half = sb("half", [P, NT])
        one1 = sb("one1", [P, 1])

        X = sb("X", [P, NT, C])
        XN = sb("XN", [P, NT, C])
        XT = sb("XT", [P, T])
        ST_ = sb("ST_", [P, NT, 6])
        MV = sb("MV", [P, NT, 2])
        VE = sb("VE", [P, NT])
        RS = sb("RS", [P, NT])
        SB = sb("SB", [P, NT, C])
        GB = sb("GB", [P, NT, C])
        U = sb("U", [P, RING * 4 * T])
        ring = lambda i: U[:, (i % RING) * 4 * T:(i % RING + 1) * 4 * T]
        stT = U[:, 4 * 4 * T:4 * 4 * T + 2 * T].rearrange("p (h t) -> p h t", h=2)
        band = [U[:, i * NH * BAND:(i + 1) * NH * BAND].rearrange("p (n t) -> p n t", n=NH) for i in range(NT)]
        UB = U[:, :].bitcast(BF16)
        QS = UB[:, 0:NH * T].rearrange("p (n t) -> p n t", n=NH)
        KS = UB[:, NH * T:2 * NH * T].rearrange("p (n t) -> p n t", n=NH)
        wslot = [U[:, s + 2 * FF * i:s + 2 * FF * (i + 1)].rearrange("p (k f) -> p k f", k=2)
                 for s in (NH * T // 4, 3 * NH * T // 4, NH * T) for i in range(2)][0:WSLOTS]
        QSG, KSG = [UB[:, (2 * RING - 1) * 2 * T * 2 + 8 * P * i:(2 * RING - 1) * 2 * T * 2 + 8 * P * (i + 1)]
                    .rearrange("p (n t) -> p n t", n=8) for i in range(2)]
        nat = U[:, 0:NTILE * P].rearrange("p (k c) -> p k c", k=NTILE)
        D = sb("D", [P, 8 * T + 256])
        BS = D[:, 0:4 * T].rearrange("p (g t) -> p g t", g=4)
        DS = D[:, 4 * T:8 * T].rearrange("p (g t) -> p g t", g=4)
        WA = D[:, 0:2 * (T + PAD)].rearrange("p (h t) -> p h t", h=2)
        WB = D[:, 2 * (T + PAD):4 * (T + PAD)].rearrange("p (h t) -> p h t", h=2)
        MM = D[:, 4 * (T + PAD):4 * (T + PAD) + 2 * T].rearrange("p (h t) -> p h t", h=2)
        WBT = D[:, 0:4 * T].rearrange("p (j n o) -> p j n o", j=NT, n=NH)
        RC = D[:, 4 * T:6 * T].rearrange("p (h t) -> p h t", h=2)
        PT = D[:, 0:8 * T].rearrange("p (s q t) -> p s q t", s=4, q=2)
        HB = D[:, 0:8 * T].rearrange("p (s f t) -> p s f t", s=2, f=NF)
        DT = sb("DT", [P, 2, PAD + T])
        PP = sb("PP", [P, 2, PAD + T])
        EP = sb("EP", [P, 2, PAD + T])
        QE = sb("QE", [P, 2, T])
        OS = QE
        VP = sb("VP", [P, NT, NH, 32])
        MX = sb("MX", [P, NT, NH])
        LO = sb("LO", [P, NT, C])
        HT = LO[:, :, :].rearrange("p j c -> p (j c)")
        MT = HT[0:16, :]
        M8 = sb("M8", [P, NT, 8])
        MG = sb("MG", [P, NT, 8, 8])
        SCO = sb("SCO", [P, NT, 64])
        RPL = sb("RPL", [P, NT, 64])
        MSK = RPL
        DIF = sb("DIF", [P, NT, 64])
        GT = sb("GT", [P, NT, 64])
        GS = sb("GS", [P, NT, 8])
        GM = sb("GM", [P, NT, 8])
        SM = sb("SM", [P, NT])
        GX = sb("GX", [1, P])
        GC = sb("GC", [P, 1])
        F = EP[:, :, PAD:]
        SPL = D[:, 0:3 * T].bitcast(BF16).rearrange("p (a k t) -> p a k t", a=2, k=3)
        NMF = sb("NMF", [P, NT, NH])
        NM = sb("NM", [P, NT, 3 * NH], BF16)
        NMT = sb("NMT", [3 * NH, T], BF16)
        CGT = sb("CGT", [LD, P])
        GO = sb("GO", [P, LD])
        PR = sb("PR", [P, NT, 2])
        SCT = EP[0:E1, 0, PAD:]
        KV = D[:, 0:NT * 2 * C].rearrange("p (j k c) -> p j k c", j=NT, k=2)
        KVT = D[:, 1024:1024 + C]
        KVO = D[:, 1280:1280 + C + 1]
        CB = U[:, NH * T:NH * T + NT * 96].bitcast(BF16).rearrange("p (j n) -> p j n", j=NT)
        CT = U[:, NH * T + T:NH * T + 2 * T].bitcast(BF16).rearrange("p (k t) -> p k t", k=2)
        SPLG = PP[:, 0, PAD:PAD + 3 * P].bitcast(BF16).rearrange("p (a k t) -> p a k t", a=2, k=3)
        SC8 = GB[0:E1, :, :].rearrange("p j c -> p (j c)")
        SL = DT[:, :, PAD:]
        AV = PP[:, :, PAD:]
        PSall = ctx.enter_context(nc.psum_tensor("PS", [P, 8, T], FP32))
        PS = lambda k: PSall[:, k, :]
        PSB = lambda k: PSall[:, k, :].bitcast(BF16)
        loaded = {}

        def sp_prologue(e):
            def load(dst, src, name):
                e.dma_start(dst, src, allow_slow_non_contiguous=True).then_inc(S[name], 16)
                loaded[name] = loaded.get(name, 0) + 16
            load(CN[:, :], a["consts"], "w_consts")
            e.wait_ge(S["nat_zero"], 1)
            load(nat[0:8, T_GATES, :], a["L0_ffn_router_w"], "w_nat")
            load(nat[8:24, T_GATES, :], a["L2_ffn_gate_w"], "w_nat")
            load(nat[24:88, T_GATES, :], a["L3_ffn_gate_w"], "w_nat")
            load(nat[:, T_LD, :], a["L0_ffn_lora_down"].rearrange("e r h -> (e r) h"), "w_nat")
            load(nat[:, T_LU, :].rearrange("p (e r) -> p e r", e=8), a["L0_ffn_lora_up"].rearrange("e h r -> h e r"), "w_nat")
            load(nat[:, T_QKV:T_QKV + 3, :], a["L2_attn_W_qkv"].rearrange("(k p) c -> p k c", p=P), "w_nat")
            load(nat[:, T_WO2, :], a["L2_attn_W_out"], "w_nat")
            load(nat[:, T_W1:T_W1 + 8, :], a["L2_ffn_w1"].rearrange("(k e) h c -> (e h) k c", e=2), "w_nat")
            load(nat[:, T_W3:T_W3 + 8, :], a["L2_ffn_w3"].rearrange("(k e) h c -> (e h) k c", e=2), "w_nat")
            load(nat[:, T_W2:T_W2 + 8, :].rearrange("p k (e h) -> p (k e) h", e=2), a["L2_ffn_w2"].rearrange("e d h -> d e h"), "w_nat")
            load(nat[0:64, T_SW13, :], a["L2_ffn_sw1"], "w_nat")
            load(nat[64:128, T_SW13, :], a["L2_ffn_sw3"], "w_nat")
            load(nat[:, T_SW2, 0:64], a["L2_ffn_sw2"], "w_nat")
            load(nat[0:32, T_B, :], a["L1_ffn_b1"].rearrange("e (f p) -> (e f) p", p=P), "w_nat")
            load(nat[32:36, T_B, :], a["L1_ffn_rb1"].rearrange("(f p) -> f p", p=P), "w_nat")
            load(nat[36:38, T_B, :], a["L0_attn_b_disp"].rearrange("(f p) -> f p", p=P), "w_nat")
            load(nat[38:39, T_B, :], a["L3_attn_bq"].rearrange("(o h) k -> o (h k)", o=1), "w_nat")
            load(nat[39:40, T_B, :], a["L3_attn_bk"].rearrange("(o h) k -> o (h k)", o=1), "w_nat")
            load(nat[40:41, T_B, 0:64], a["L1_attn_b_lqkv"].rearrange("(o h) -> o h", o=1)[:, 0:64], "w_nat")
            load(nat[41:42, T_B, 0:64], a["L1_attn_b_lqkv"].rearrange("(o h) -> o h", o=1)[:, 64:128], "w_nat")
            load(nat[42:43, T_B, 0:64], a["L1_attn_b_gqkv"].rearrange("(o h) -> o h", o=1)[:, 0:64], "w_nat")
            load(nat[43:44, T_B, 0:64], a["L1_attn_b_gqkv"].rearrange("(o h) -> o h", o=1)[:, 64:128], "w_nat")
            load(nat[44:45, T_B, 0:64], a["L1_attn_b_comp"].rearrange("(o h) -> o h", o=1)[:, LD:C], "w_nat")
            for k, n in enumerate(("strain", "state", "state_i", "state_j", "damage", "pos")):
                load(W16[:, 16 * k:16 * k + 16], a[f"L0_attn_w_{n}"], "w_small")
            for k, n in enumerate(("b_state", "b_strain", "b_damage")):
                load(W16[:, 96 + k:97 + k], a[f"L0_attn_{n}"].rearrange("(k o) -> k o", o=1), "w_small")
            load(W16[:, 99:100], a["L0_attn_w_bond_out"], "w_small")
            load(W16[:, 100:101], a["L0_attn_w_damage_out"], "w_small")
            load(W16[:, 104:136], a["L0_attn_rel_pos_emb"].rearrange("h k -> k h"), "w_small")
            load(SC1[:, 0:1], a["L0_attn_b_bond_out"].partition_broadcast(P), "w_small")
            load(SC1[:, 2:3], a["L0_attn_b_damage_out"].partition_broadcast(P), "w_small")
            load(wdisp[:, :], a["L0_attn_w_disp"], "w_small")
            load(wval[:, :], a["L0_attn_w_val"], "w_small")
            load(WCPN[:, :], a["L0_attn_w_cproj"], "w_small")
            load(WON[:, :], a["L3_attn_Wo"].rearrange("h k d -> (h k) d"), "w_small")
            load(WLG[:, 0, :], a["L1_attn_w_lproj"], "w_small")
            load(WLG[:, 1, :], a["L1_attn_w_gproj"], "w_small")
            load(wqkv1[:, 0, :], a["L1_attn_w_lqkv"], "w_small")
            load(wqkv1[:, 1, :], a["L1_attn_w_gqkv"], "w_small")
            load(wcomp[:, :, :], a["L1_attn_w_comp"].rearrange("(r p) c -> p r c", p=P)[:, :, LD:C], "w_small")
            row = lambda k: a[k].partition_broadcast(P)
            load(rc["b_val"], row("L0_attn_b_val"), "w_small")
            load(rc["b_cproj"], row("L0_attn_b_cproj"), "w_small")
            load(rc["b_lproj"], row("L1_attn_b_lproj"), "w_small")
            load(rc["b_gproj"], row("L1_attn_b_gproj"), "w_small")
            load(rc["w_gate"], a["L1_attn_w_gate"].rearrange("c g -> (c g)").partition_broadcast(P), "w_small")
            load(rc["b_gate"], row("L1_attn_b_gate"), "w_small")
            load(rc["b_out"], row("L2_attn_b_out"), "w_small")
            load(rc["bv"], a["L3_attn_bv"].rearrange("h k -> (h k)").partition_broadcast(P), "w_small")
            load(rc["gate_bias"], row("L3_ffn_gate_bias"), "w_small")
            load(rc["bvl"], a["L1_attn_b_lqkv"][2 * LD:3 * LD].partition_broadcast(P), "w_small")
            load(rc["bvg"], a["L1_attn_b_gqkv"][2 * LD:3 * LD].partition_broadcast(P), "w_small")
            load(rw1[:, :], a["L1_ffn_rw1"], "w_small")
            load(rw2[:, :, :], a["L1_ffn_rw2"].rearrange("(f p) e -> p f e", p=P), "w_small")
            load(rb2[:, :], a["L1_ffn_rb2"].rearrange("(e o) -> e o", o=1), "w_small")
            load(b2[:, :], a["L1_ffn_b2"], "w_small")
            for k, n in enumerate(("Wq", "Wk", "Wv")):
                load(wqkv3[:, k, :, :], a[f"L3_attn_{n}"].rearrange("h d k -> d h k"), "w_small")
            e.wait_ge(S["zero_ready"], 1)
            zeros = D[:, 0:NH * BAND].rearrange("p (n t) -> p n t", n=NH)
            for j in range(NT):
                load(z_dram[j].rearrange("n p t -> p n t"), zeros, "scratch_zero")
            load(e_dram[:, :, T:T + HOR], D[:, 0:4 * HOR].rearrange("p (g t) -> p g t", g=4), "scratch_zero")

        def act_late_loads(e):
            e.dma_start(WS3[:, 0, :], a["L3_ffn_Ws_gate"]).then_inc(S["w_late"], 16)
            e.dma_start(WS3[:, 1, :], a["L3_ffn_Ws_up"]).then_inc(S["w_late"], 16)
            e.dma_start(WSD3[:, :], a["L3_ffn_Ws_down"]).then_inc(S["w_late"], 16)
            e.dma_start(WG3[:, :, :], a["L3_ffn_We_gate"].rearrange("e h f -> h e f")).then_inc(S["w_late"], 16)
            e.dma_start(WU3[:, :, :], a["L3_ffn_We_up"].rearrange("e h f -> h e f")).then_inc(S["w_late"], 16)
            e.dma_start(WD3[:, :, :], a["L3_ffn_We_down"].rearrange("(k e) f h -> (e f) k h", e=2)).then_inc(S["w_late"], 16)
            loaded["w_late"] = 96

        def pool_prologue(e):
            e.memset(nat[:, T_GATES, :], 0.0).then_inc(S["pool_pro"], 1)
            e.memset(nat[:, T_SW2, :], 0.0).then_inc(S["pool_pro"], 1)
            e.memset(nat[:, T_B:T_B + 3, :], 0.0).then_inc(S["pool_pro"], 1)
            e.wait_ge(S["pool_pro"], 3)
            e.memset(one1[:, :], 1.0).then_inc(S["nat_zero"], 1)
            e.memset(D[:, :], 0.0).then_inc(S["zero_ready"], 1)
            e.memset(half[:, :], -0.5).then_inc(S["pool_pro"], 1)
            e.memset(VP[:, :, :, :], 0.0).then_inc(S["pool_pro"], 1)
            e.memset(DT[:, :, 0:PAD], 0.0).then_inc(S["pool_pro"], 1)
            e.memset(PP[:, :, 0:PAD], 0.0).then_inc(S["pool_pro"], 1)
            e.memset(EP[:, :, 0:PAD], 0.0).then_inc(S["pool_pro"], 1)
            e.memset(ONEZ[:, 0, :], 0.0).then_inc(S["pool_pro"], 1)
            e.memset(ONEZ[:, 1, :], 1.0).then_inc(S["pool_pro"], 1)
            e.wait_ge(S["pool_pro"], 10)
            for r in range(2):
                v = VP[:, :, :, :].rearrange("p j (m r) c -> p j m r c", r=2)
                e.memset(v[:, :, :, r, 16 * r + 8], 1.0).then_inc(S["pool_pro"], 1)
            e.wait_ge(S["pool_pro"], 12)

        def pe_prologue(e):
            e.wait_ge(S["w_consts"], loaded["w_consts"])
            e.wait_ge(S["w_nat"], loaded["w_nat"])
            for k in range(NTILE - 2):
                if k >= 32 and k % 4 == 0:
                    e.wait_ge(S["wt_out"], k // 4 - 7)
                last = e.transpose(PSall[:, k // 4 % 8, k % 4 * P:k % 4 * P + P], nat[:, k, :], ident)
                if k % 4 == 3 or k == NTILE - 3:
                    last.then_inc(S["wt_ready"], 1)
            e.wait_ge(S["w_small"], loaded["w_small"])
            e.wait_ge(S["wt_out"], 9)
            rep = cn("rep16")[0:16, :]
            e.matmul(PS(0)[:, 0:101], rep, W16[:, 0:101], start=True, stop=True).then_inc(S["pro_mm"], 1)
            e.matmul(PS(1)[0:16, 0:HOR], W16[:, 80:96], W16[:, 104:136], start=True, stop=True).then_inc(S["pro_mm"], 1)
            for h in range(2):
                sel = cn(f"pad_sel{h}")
                e.matmul(PS(2)[:, P * h:P * h + P], sel, WCPN[:, :], start=(h == 0), stop=(h == 1), skip_group_check=True)
                last = e.matmul(PS(3)[:, P * h:P * h + P], sel, WON[:, :], start=(h == 0), stop=(h == 1), skip_group_check=True)
            for k in range(2):
                last = e.matmul(PS(4)[:, LD * k:LD * k + LD], cn("pad_sel0")[0:LD, :], WLG[:, k, :], start=(k == 0), stop=(k == 1), skip_group_check=True)
            last.then_inc(S["pro_mm"], 1)
            e.wait_ge(S["rd16"], 1)
            e.matmul(PS(5)[:, 0:HOR], rep, RD16[:, :], start=True, stop=True).then_inc(S["pro_mm"], 1)

        def act_prologue(e):
            for k in range(9):
                e.wait_ge(S["wt_ready"], k + 1)
                n = min(4, NTILE - 2 - 4 * k)
                e.activation(WT[:, 4 * k:4 * k + n, :], PS(k % 8)[:, 0:n * P].rearrange("p (k c) -> p k c", c=P), ACT.Copy).then_inc(S["wt_out"], 1)
            e.wait_ge(S["pro_mm"], 3)
            e.activation(WCP[:, :, :], PS(2)[:, 0:2 * P].rearrange("p (k c) -> p k c", k=2), ACT.Copy).then_inc(S["act_pro"], 1)
            e.activation(WOP[:, :, :], PS(3)[:, 0:2 * P].rearrange("p (k c) -> p k c", k=2), ACT.Copy).then_inc(S["act_pro"], 1)
            e.activation(WLGP[:, :, :], PS(4)[:, 0:2 * LD].rearrange("p (k c) -> p k c", k=2), ACT.Copy).then_inc(S["act_pro"], 1)
            e.wait_ge(S["wt_out"], 9)
            e.wait_ge(S["act_pro"], 3)

        def dve_prologue(e):
            e.wait_ge(S["w_consts"], loaded["w_consts"])
            e.tensor_copy(identb[:, :], ident).then_inc(S["dve_pro"], 1)
            e.tensor_copy(maskb[:, 0, :], cn("causal_qk")).then_inc(S["dve_pro"], 1)
            e.tensor_copy(maskb[:, 1, :], cn("causal_kq")).then_inc(S["dve_pro"], 1)
            e.tensor_copy(hot64b[:, :], cn("hot64")).then_inc(S["dve_pro"], 1)
            e.tensor_copy(hot16b[:, :], cn("hot16")[0:48, :]).then_inc(S["dve_pro"], 1)
            e.wait_ge(S["pro_mm"], 2)
            e.tensor_copy(RD16[:, :], PS(1)[0:16, 0:HOR]).then_inc(S["rd16"], 1)
            e.tensor_copy(REP[:, 0:101 - 5], PS(0)[:, 0:96]).then_inc(S["dve_pro"], 1)
            e.tensor_copy(BVC[:, :], PS(0)[:, 96:101]).then_inc(S["dve_pro"], 1)
            e.wait_ge(S["dve_pro"], 7)
            blk = cn("block16").unsqueeze(2).broadcast_to([P, 8, 16])
            for k in range(5):
                e.tensor_tensor(BDM[:, k, :, :], REP[:, 16 * k:16 * k + 16].unsqueeze(1).broadcast_to([P, 8, 16]), blk, ALU.mult).then_inc(S["dve_pro"], 1)
            for k in range(2):
                e.tensor_scalar(WOUT[:, k, :, :].rearrange("p c n -> p (c n)"), cn("slot_mask"), BVC[:, 3 + k:4 + k], None, ALU.mult).then_inc(S["dve_pro"], 1)
            e.wait_ge(S["w_small"], loaded["w_small"])
            e.tensor_scalar(SC1[:, 1:2], SC1[:, 2:3], 0.5, None, ALU.mult).then_inc(S["dve_pro"], 1)
            e.tensor_scalar(SC1[:, 3:4], SC1[:, 0:1], -5.0, None, ALU.add).then_inc(S["dve_pro"], 1)
            wg = rc["w_gate"].rearrange("p (c g) -> p c g", g=2)
            e.tensor_tensor(WDIF[:, 0:C], wg[:, :, 0], wg[:, :, 1], ALU.subtract).then_inc(S["dve_pro"], 1)
            e.tensor_tensor(WDIF[:, C:C + 1], rc["b_gate"][:, 0:1], rc["b_gate"][:, 1:2], ALU.subtract).then_inc(S["dve_pro"], 1)
            e.wait_ge(S["dve_pro"], 18)
            e.tensor_scalar(BDM[:, 5, :, :].rearrange("p a b -> p (a b)"), BDM[:, 0, :, :].rearrange("p a b -> p (a b)"), -1.0, None, ALU.mult).then_inc(S["dve_pro"], 1)
            e.wait_ge(S["pro_mm"], 4)
            e.tensor_scalar(RD[:, :], PS(5)[:, 0:HOR], BVC[:, 1:2], None, ALU.add).then_inc(S["dve_pro"], 1)
            e.wait_ge(S["dve_pro"], 20)

        def ready(e):
            e.wait_ge(S["w_consts"], loaded["w_consts"])
            e.wait_ge(S["w_nat"], loaded["w_nat"])
            e.wait_ge(S["w_small"], loaded["w_small"])
            e.wait_ge(S["pool_pro"], 12)
            e.wait_ge(S["nat_zero"], 1)
            e.wait_ge(S["wt_out"], 9)
            e.wait_ge(S["act_pro"], 3)
            e.wait_ge(S["dve_pro"], 20)
            e.wait_ge(S["rd16"], 1)
            e.wait_ge(S["scratch_zero"], loaded["scratch_zero"])

        bd = lambda k: BDM[:, k, :, :].rearrange("p a b -> p (a b)")
        bcol = lambda k: WT[:, T_B, k:k + 1]

        def dve_norm(e, b, l, step):
            b = stage_turn(e, b)
            for j in range(NT):
                last = e.bn_stats(ST_[:, j, :], X[:, j, :])
            step(last, alone=True)
            for j in range(NT):
                last = e.bn_aggr(MV[:, j, :], ST_[:, j, :])
            step(last)
            e.tensor_scalar(VE[:, :], MV[:, :, 1], LN_EPS, None, ALU.add).then_inc(S["var"], 1)
            e.wait_ge(S["rstd"], at("rstd", b, l + 1))
            for j in range(NT):
                last = e.tensor_scalar(XN[:, j, :], X[:, j, :], MV[:, j, 0:1], RS[:, j:j + 1], ALU.subtract, ALU.mult)
            last.then_inc(S["xn"], 1)

        def pool_norm(e, b, l):
            b = stage_turn(e, b)
            e.wait_ge(S["var"], at("var", b, l + 1))
            e.tensor_tensor(RS[:, :], VE[:, :], half[:, :], ALU.pow).then_inc(S["rstd"], 1)

        def pe_norm(e, b, l):
            b = stage_turn(e, b)
            e.wait_ge(S["xn"], at("xn", b, l + 1))
            for j in range(NT):
                last = e.transpose(PS(0)[:, P * j:P * j + P], XN[:, j, :], ident)
            last.then_inc(S["xt_ps"], 1)

        def act_norm(e, b, l):
            b = stage_turn(e, b)
            e.wait_ge(S["xt_ps"], at("xt_ps", b, l + 1))
            e.activation(XT[:, :], PS(0), ACT.Copy).then_inc(S["xt"], 1)

        POOL_ITEMS = [i for i in range(32) if i % 8 < 4 and i not in (0, 1, 2, 8, 9, 16, 17, 24)]

        def item(i):
            g, k = i // 8, i % 8
            return g, g // 2, g % 2, k % 4, k // 4

        def damage_add(e, i):
            g, u, h, c, _ = item(i)
            src = EP[:, h, :]
            start = PAD - 16 * u - 12 - c
            win = bass.AP(src.tensor, src.offset + start, [list(src.ap[0]), [4, 4], [1, T]])
            return e.tensor_tensor(ring(i).rearrange("p (q t) -> p q t", q=4), win,
                                   QE[:, h, :].unsqueeze(1).broadcast_to([P, 4, T]), ALU.add)

        def pe_l0(e, b):
            b = stage_turn(e, b)
            e.wait_ge(S["xt"], at("xt", b, 1))
            for h in range(2):
                e.matmul(PS(4 + h), wdisp[:, P * h:P * h + P], XT[:, :], start=True, stop=True).then_inc(S["disp_ps"], 1)
            for j in range(NT):
                last = e.matmul(PS(6)[:, P * j:P * j + P], XT[:, P * j:P * j + P], wval[:, :], start=(j == 0), stop=(j == NT - 1), skip_group_check=True)
            last.then_inc(S["val_ps"], 1)
            for h in range(2):
                e.wait_ge(S["disp"], at("disp", b, h + 1))
                e.matmul(PS(2 + h), bd(4), DT[:, h, PAD:], start=True, stop=True).then_inc(S["dam_ps"], 1)
            for h in range(2):
                e.wait_ge(S["wmean"], at("wmean", b, 1))
                e.matmul(PS(4 + h), bd(1), MM[:, h, :], start=True, stop=True).then_inc(S["state_ps"], 1)
            e.wait_ge(S["val"], at("val", b, 1))
            for h in range(2):
                e.wait_ge(S["state"], at("state", b, h + 1))
                e.wait_ge(S["dam"], at("dam", b, h + 1))
                e.matmul(PS(2 + h), bd(0), DT[:, h, PAD:], start=True, stop=False)
                e.matmul(PS(2 + h), bd(3), stT[:, h, :], start=False, stop=True).then_inc(S["p_ps"], 1)
                e.matmul(PS(6 + h), bd(5), DT[:, h, PAD:], start=True, stop=False)
                e.matmul(PS(6 + h), bd(2), stT[:, h, :], start=False, stop=True).then_inc(S["q_ps"], 1)
            for i in range(32):
                g, u, h, c, kind = item(i)
                bank = g % 2 + 4 * kind
                if c == 0 and g >= 2:
                    e.wait_ge(S["logit_out"], at("logit_out", b, 2 * (g - 2) + kind + 1))
                e.wait_ge(S["act"], at("act", b, i + 1))
                for x in range(4):
                    q = 3 - x
                    last = e.matmul(PS(bank)[32 * q:32 * q + 32, :], WOUT[:, 1 - kind, c, :], ring(i)[:, T * x:T * x + T],
                                    start=(c == 0), stop=(c == 3))
                last.then_inc(S["act_used"], 1)
            e.wait_ge(S["logit"], at("logit", b, 1))
            for j in range(NT):
                for h in range(2):
                    for u in range(2):
                        last = e.transpose(PS(j)[:, 256 * h + 128 * u:256 * h + 128 * u + P], BS[:, 2 * u + h, P * j:P * j + P], ident)
                last.then_inc(S["logit_t"], 1)
            for j in range(NT):
                e.wait_ge(S["lmax"], at("lmax", b, j + 1))
                last = e.transpose(PS(4)[0:NH, P * j:P * j + P], MX[:, j, :], ident)
            last.then_inc(S["lmax_t"], 1)
            e.wait_ge(S["lmax_row"], at("lmax_row", b, 1))
            for h in range(2):
                e.matmul(PS(6 + h), cn(f"sel_head{h}")[0:NH, :], MT[:, :], start=True, stop=True).then_inc(S["lmax_b"], 1)
            e.wait_ge(S["skewed"], at("skewed", b, 64))
            for j in range(NT):
                for h in range(2):
                    for u in range(2):
                        last = e.transpose(PS(j)[:, 256 * h + 128 * u:256 * h + 128 * u + P], DS[:, 2 * u + h, P * j:P * j + P], ident)
                last.then_inc(S["exp_t"], 1)
            pe_f0(e, b)
            for j in range(NT):
                w = min(BAND, T - P * j)
                e.wait_ge(S[f"band{j}"], at(f"band{j}", b, 16))
                for h in range(2):
                    for r in range(2):
                        for q in range(4):
                            last = e.matmul(PS(4 + h)[32 * q:32 * q + 32, P * j:P * j + w], VP[:, j, 8 * h + 2 * q + r, :],
                                            band[j][:, 8 * h + 2 * q + r, 0:w], start=(j == 0 and r == 0),
                                            stop=(j == NT - 1 and r == 1), skip_group_check=True)
                last.then_inc(S["band_used"], 1)
            pe_heads_out(e, b, "0", 2, T, WCP, PS(0), C)

        def pe_heads_out(e, b, tag, nh, n, w, dst, width):
            b = stage_turn(e, b)
            e.wait_ge(S["os"], tagged("os", tag, b, 1))
            for h in range(nh):
                last = e.matmul(PS(2 + h)[:, 0:n], cn("sel_den"), OS[:, h, 0:n], start=True, stop=True)
            last.then_inc(S["den"], 1)
            e.wait_ge(S["on"], tagged("on", tag, b, 1))
            for j in range(n // P):
                for h in range(nh):
                    last = e.matmul(dst[:, width * j:width * j + width], OS[:, h, P * j:P * j + P], w[:, h, :],
                                    start=(j == 0 and h == 0), stop=(j == n // P - 1 and h == nh - 1), skip_group_check=True)
            last.then_inc(S["proj"], 1)

        def dve_heads_out(e, b, tag, nh, n, step):
            b = stage_turn(e, b)
            e.wait_ge(S["den"], tagged("den", tag, b, 1))
            step(e.reciprocal(RC[:, 0:nh, 0:n], PSall[:, 2:2 + nh, 0:n]))
            e.tensor_tensor(OS[:, 0:nh, 0:n], OS[:, 0:nh, 0:n], RC[:, 0:nh, 0:n], ALU.mult).then_inc(S["on"], 1)

        def act_l0(e, b):
            b = stage_turn(e, b)
            for h in range(2):
                e.wait_ge(S["disp_ps"], at("disp_ps", b, h + 1))
                e.activation(DT[:, h, PAD:], PS(4 + h), ACT.Identity, bias=bcol(36 + h)).then_inc(S["disp"], 1)
            for h in range(2):
                e.wait_ge(S["dam_ps"], at("dam_ps", b, h + 1))
                e.activation(EP[:, h, PAD:], PS(2 + h), ACT.Copy).then_inc(S["dam"], 1)
            for i in range(32):
                if i == 2:
                    for h in range(2):
                        e.wait_ge(S["state_ps"], at("state_ps", b, h + 1))
                        e.activation(stT[:, h, :], PS(4 + h), ACT.Identity, bias=BVC[:, 0:1]).then_inc(S["state"], 1)
                    for h in range(2):
                        e.wait_ge(S["p_ps"], at("p_ps", b, h + 1))
                        e.activation(PP[:, h, PAD:], PS(2 + h), ACT.Copy).then_inc(S["p_sb"], 1)
                if i in POOL_ITEMS:
                    e.wait_ge(S["pre_pool"], at("pre_pool", b, POOL_ITEMS.index(i) + 1))
                else:
                    e.wait_ge(S["pre_dve"], at("pre_dve", b, i + 1 - len([k for k in POOL_ITEMS if k < i])))
                e.activation(ring(i), ring(i), ACT.Gelu).then_inc(S["act"], 1)
            e.wait_ge(S["logit_out"], at("logit_out", b, 8))
            e.activation(D[:, 4 * T:8 * T], D[:, 4 * T:8 * T], ACT.Tanh, bias=SC1[:, 1:2], scale=0.5).then_inc(S["damage"], 1)
            e.wait_ge(S["shifted"], at("shifted", b, 1))
            e.activation(D[:, 0:4 * T], D[:, 0:4 * T], ACT.Exp).then_inc(S["lexp"], 1)
            e.wait_ge(S["e_stored"], at("e_stored", b, 16))
            for j in range(NT):
                e.wait_ge(S["exp_t"], at("exp_t", b, j + 1))
                src = PS(j).rearrange("p (h o n) -> p h n o", h=2, o=HOR)
                e.activation(WBT[:, j, :, :].rearrange("p (h n) o -> p h n o", h=2), src, ACT.Copy).then_inc(S["by_key"], 1)
            act_f0(e, b)
            e.wait_ge(S["band_used"], at("band_used", b, 4))
            e.activation(OS[:, :, :], PSall[:, 4:6, :], ACT.Copy).then_inc(S["os"], 1)

        def pool_l0(e, b):
            b = stage_turn(e, b)
            wait_alone(e, at("disp", b, 2))
            e.wait_ge(S["disp"], at("disp", b, 2))
            e.memset(D[:, 0:4 * (T + PAD)].rearrange("p (k t) -> p k t", k=4)[:, :, 0:PAD], 0.0).then_inc(S["wsum"], 1)
            src = DT
            for k, (sh, dst) in enumerate(((1, WA), (2, WB), (4, WA), (8, WB), (16, WA))):
                e.wait_ge(S["wsum"], at("wsum", b, k + 1))
                e.tensor_tensor(dst[:, :, PAD:], src[:, :, PAD:], src[:, :, PAD - sh:PAD - sh + T], ALU.add).then_inc(S["wsum"], 1)
                src = dst
            e.wait_ge(S["wsum"], at("wsum", b, 6))
            e.tensor_tensor(WA[:, :, PAD:2 * PAD], WA[:, :, PAD:2 * PAD], cn("count_fix").unsqueeze(1).broadcast_to([P, 2, PAD]), ALU.mult).then_inc(S["wsum"], 1)
            for n, i in enumerate(POOL_ITEMS):
                if n == 0:
                    e.wait_ge(S["qe"], at("qe", b, 1))
                    e.wait_ge(S["dam"], at("dam", b, 2))
                if i >= RING:
                    e.wait_ge(S["act_used"], at("act_used", b, i - RING + 1))
                damage_add(e, i).then_inc(S["pre_pool"], 1)

        def dve_l0(e, b, step):
            b = stage_turn(e, b)
            e.wait_ge(S["val_ps"], at("val_ps", b, 1))
            for r in range(2):
                v = VP[:, :, :, :].rearrange("p j (m r) c -> p j m r c", r=2)[:, :, :, r, 16 * r:16 * r + 8]
                for j in range(NT):
                    ps = PS(6)[:, P * j:P * j + P].rearrange("p (m r c) -> p m r c", r=2, c=HD)[:, :, r, :]
                    bv = rc["b_val"].rearrange("p (m r c) -> p m r c", r=2, c=HD)[:, :, r, :]
                    last = e.tensor_tensor(v[:, j, :, :], ps, bv, ALU.add)
            last.then_inc(S["val"], 1)
            e.wait_ge(S["dam"], at("dam", b, 2))
            e.tensor_scalar(QE[:, :, :], EP[:, :, PAD:], -1.0, BVC[:, 2:3], ALU.mult, ALU.add).then_inc(S["qe"], 1)
            e.wait_ge(S["qe"], at("qe", b, 1))
            done = 0

            def dve_item(i):
                g, u, h, c, kind = item(i)
                if i >= RING:
                    e.wait_ge(S["act_used"], at("act_used", b, i - RING + 1))
                if kind == 0:
                    damage_add(e, i).then_inc(S["pre_dve"], 1)
                    return
                if i == 4:
                    e.wait_ge(S["p_sb"], at("p_sb", b, 2))
                    e.wait_ge(S["q_ps"], at("q_ps", b, 2))
                for x in range(4):
                    o = 16 * u + 4 * (3 - x) + c
                    last = e.scalar_tensor_tensor(out=ring(i)[:, T * x:T * x + T], in0=PP[:, h, PAD - o:PAD - o + T],
                                                  scalar=RD[:, HOR - 1 - o:HOR - o], in1=PS(6 + h), op0=ALU.add, op1=ALU.add)
                last.then_inc(S["pre_dve"], 1)

            def logit_out(g, kind):
                e.wait_ge(S["act_used"], at("act_used", b, 8 * g + 4 * kind + 4))
                if kind == 0:
                    e.tensor_copy(DS[:, g, :], PS(g % 2)).then_inc(S["logit_out"], 1)
                else:
                    e.tensor_scalar(BS[:, g, :], PS(4 + g % 2), SC1[:, 3:4], None, ALU.add).then_inc(S["logit_out"], 1)

            own = [i for i in range(32) if i not in POOL_ITEMS]
            for i in own:
                if i == 4:
                    e.wait_ge(S["wsum"], at("wsum", b, 7))
                    e.scalar_tensor_tensor(out=MM, in0=WA[:, :, PAD:], scalar=1.0 / HOR, in1=DT[:, :, PAD:], op0=ALU.mult, op1=ALU.subtract).then_inc(S["wmean"], 1)
                dve_item(i)
                for g in range(4):
                    for kind in range(2):
                        due = 8 * g + 4 * kind + 3 + 3
                        if i >= due and (g, kind) == (done // 2, done % 2):
                            if g == 0 and kind == 0:
                                e.wait_ge(S["state_ps"], at("state_ps", b, 2))
                            logit_out(g, kind)
                            done += 1
            while done < 8:
                logit_out(done // 2, done % 2)
                done += 1
            e.wait_ge(S["damage"], at("damage", b, 1))
            step(e.scalar_tensor_tensor(out=D[:, 0:4 * T], in0=D[:, 4 * T:8 * T], scalar=-5.0, in1=D[:, 0:4 * T], op0=ALU.mult, op1=ALU.add))
            e.tensor_tensor(BS[:, :, 0:HOR], BS[:, :, 0:HOR], cn("edge").rearrange("p (g t) -> p g t", g=4), ALU.add).then_inc(S["logit"], 1)
            for j in range(NT):
                e.wait_ge(S["logit_t"], at("logit_t", b, j + 1))
                e.tensor_reduce(MX[:, j, :].rearrange("p (h n) -> p h n", h=2), PS(j).rearrange("p (h o n) -> p h n o", h=2, o=HOR), AX.X, ALU.max).then_inc(S["lmax"], 1)
            e.wait_ge(S["lmax_t"], at("lmax_t", b, 1))
            e.tensor_copy(MT[:, :], PS(4)[0:NH, :]).then_inc(S["lmax_row"], 1)
            e.wait_ge(S["lmax_b"], at("lmax_b", b, 2))
            for u in range(2):
                last = e.tensor_tensor(BS[:, 2 * u:2 * u + 2, :], BS[:, 2 * u:2 * u + 2, :], PSall[:, 6:8, :], ALU.subtract)
            last.then_inc(S["shifted"], 1)
            dve_f0(e, b, step)
            dve_heads_out(e, b, "0", 2, T, step)
            e.wait_ge(S["proj"], tagged("proj", "0", b, 1))
            e.tensor_tensor(SB[:, :, :], PS(0).rearrange("p (j c) -> p j c", j=NT), rc["b_cproj"].unsqueeze(1).broadcast_to([P, NT, C]), ALU.add).then_inc(S["s0"], 1)
            e.wait_ge(S["s0"], at("s0", b, 1))

        def sp_l0(e, b):
            b = stage_turn(e, b)
            e.wait_ge(S["lexp"], at("lexp", b, 1))
            e.dma_start(e_dram[:, :, 0:T], BS).then_inc(S["e_stored"], 16)
            e.wait_ge(S["e_stored"], at("e_stored", b, 16))
            for u in range(2):
                for h in range(2):
                    g, row = 2 * u + h, 4 * (T + HOR)
                    src = bass.AP(e_dram.tensor, g * (T + HOR) + 16 * u, [[8 * row + 1, 16], [row, 8], [1, T]])
                    e.dma_start(DS[:, g, :], src).then_inc(S["skewed"], 16)
            for j in range(NT):
                e.wait_ge(S["by_key"], at("by_key", b, j + 1))
                dst = bass.AP(z_dram.tensor, j * NH * P * BAND, [[BAND + 1, P], [P * BAND, NH], [1, HOR]])
                e.dma_start(dst, WBT[:, j, :, :]).then_inc(S[f"z_stored{j}"], 16)
            for j in range(NT):
                e.wait_ge(S[f"z_stored{j}"], at(f"z_stored{j}", b, 16))
                e.dma_start(band[j], z_dram[j].rearrange("n p t -> p n t")).then_inc(S[f"band{j}"], 16)

        def pe_f0(e, b):
            b = stage_turn(e, b)
            e.matmul(PS(4)[0:1, 0:8], XT[:, 0:1], WT[:, T_GATES, 0:8], start=True, stop=True).then_inc(S["f0_ps"], 1)
            e.wait_ge(S["f0_sb"], at("f0_sb", b, 1))
            e.matmul(PS(5)[:, 0:1], GX[:, :], one1[0:1, :], start=True, stop=True).then_inc(S["f0_ps"], 1)
            e.matmul(PS(6), WT[:, T_LD, :], XT[:, :], start=True, stop=True).then_inc(S["f0_ps"], 1)
            e.wait_ge(S["f0_sb"], at("f0_sb", b, 2))
            for j in range(NT):
                last = e.matmul(PS(7)[:, P * j:P * j + P], HT[:, P * j:P * j + P], WT[:, T_LU, :], start=(j == 0), stop=(j == NT - 1), skip_group_check=True)
            last.then_inc(S["f0_ps"], 1)

        def dve_f0(e, b, step):
            b = stage_turn(e, b)
            e.wait_ge(S["f0_ps"], at("f0_ps", b, 1))
            step(e.tensor_copy(SCO[0:1, 0, 0:8], PS(4)[0:1, 0:8]), alone=True)
            dve_topk(e, b, "g0", 1, 1, 8, 2, step)
            e.tensor_copy(GX[0:1, :].rearrange("p (e r) -> p e r", e=8), GT[0:1, 0, 0:8].unsqueeze(2).broadcast_to([1, 8, 16])).then_inc(S["f0_sb"], 1)
            e.wait_ge(S["f0_ps"], at("f0_ps", b, 2))
            step(e.tensor_copy(GC[:, :], PS(5)[:, 0:1]))
            e.wait_ge(S["f0_ps"], at("f0_ps", b, 3))
            e.tensor_scalar(HT[:, :], PS(6), GC[:, 0:1], None, ALU.mult).then_inc(S["f0_sb"], 1)
            e.wait_ge(S["f0_ps"], at("f0_ps", b, 4))
            e.tensor_tensor(GB[:, :, :], PS(7).rearrange("p (j c) -> p j c", j=NT), XN[:, :, :], ALU.add).then_inc(S["f"], 1)

        def dve_topk(e, b, tag, p, nt, ne, k, step):
            b = stage_turn(e, b)
            for j in range(nt):
                last = e.max(M8[0:p, j, :], SCO[0:p, j, 0:ne])
            step(last)
            e.tensor_tensor(DIF[0:p, 0:nt, 0:ne], SCO[0:p, 0:nt, 0:ne], M8[0:p, 0:nt, 0:1].broadcast_to([p, nt, ne]), ALU.subtract).then_inc(S["best_dif"], 1)
            e.wait_ge(S["best_dif"], at("best_dif", b, int(tag[1]) + 1))
            step(e.memset(M8[0:p, 0:nt, k:8], GONE), alone=True)
            for j in range(nt):
                last = e.match_replace(RPL[0:p, j, 0:ne], M8[0:p, j, :], SCO[0:p, j, 0:ne], GONE)
            step(last)
            step(e.tensor_scalar(MSK[0:p, 0:nt, 0:ne], RPL[0:p, 0:nt, 0:ne], GONE / 2, None, ALU.is_le))
            e.wait_ge(S["best_exp"], at("best_exp", b, int(tag[1]) + 1))
            step(e.tensor_tensor(GT[0:p, 0:nt, 0:ne], DIF[0:p, 0:nt, 0:ne], MSK[0:p, 0:nt, 0:ne], ALU.mult))
            step(e.tensor_reduce(SM[0:p, 0:nt], GT[0:p, 0:nt, 0:ne], AX.X, ALU.add))
            step(e.reciprocal(SM[0:p, 0:nt], SM[0:p, 0:nt]))
            step(e.tensor_tensor(GT[0:p, 0:nt, 0:ne], GT[0:p, 0:nt, 0:ne], SM[0:p, 0:nt].unsqueeze(2).broadcast_to([p, nt, ne]), ALU.mult))

        def act_topk(e, b, tag, p, nt, ne):
            b = stage_turn(e, b)
            e.wait_ge(S["best_dif"], at("best_dif", b, int(tag[1]) + 1))
            e.activation(DIF[0:p, 0:nt, 0:ne], DIF[0:p, 0:nt, 0:ne], ACT.Exp).then_inc(S["best_exp"], 1)

        def act_f0(e, b):
            b = stage_turn(e, b)
            act_topk(e, b, "g0", 1, 1, 8)
            act_gate(e, b, 0)

        def act_gate(e, b, l):
            b = stage_turn(e, b)
            e.wait_ge(S["f"], at("f", b, l + 1))
            e.activation(GB[:, :, :], GB[:, :, :], ACT.Silu).then_inc(S["gate"], 1)

        def dve_update(e, b, l, step):
            b = stage_turn(e, b)
            e.wait_ge(S["gate"], at("gate", b, l + 1))
            step(e.tensor_tensor(SB[:, :, :], SB[:, :, :], GB[:, :, :], ALU.mult))
            e.tensor_tensor(X[:, :, :], X[:, :, :], SB[:, :, :], ALU.add).then_inc(S["x"], 1)
            e.wait_ge(S["x"], at("x", b, l + 1))

        def attn_shape(tag):
            stacks = dict(ATTN[tag] or {}, QS=QS, KS=KS, SPL=SPL, qd=q_dram, kd=k_dram, vh=0, banks=(0, 1, 2))
            if tag == "L":
                return dict(stacks, w=wqkv1[:, 0, :], xin=XT[0:LD, :], src=("xt", 2), bc=(40, 41), bv=rc["bvl"])
            if tag == "G":
                return dict(stacks, QS=QSG, KS=KSG, SPL=SPLG, qd=qg_dram, kd=kg_dram, vh=8, banks=(7, 0, 1), w=wqkv1[:, 1, :], xin=CGT[:, :], src=("cgt", 1), bc=(42, 43), bv=rc["bvg"])
            return dict(stacks, w=wqkv3[:, :, :, :].rearrange("p a h k -> p (a h k)"), xin=XT[:, :], src=("xt", 4), bc=(38, 39), bv=rc["bv"])

        SCALE = float(HD) ** -0.5
        KTYPES = (0, 1, 2, 0, 1)

        def pe_qkv(e, b, tag):
            b = stage_turn(e, b)
            c = attn_shape(tag)
            nh, n, nt, mr = c["nh"], c["n"], c["n"] // P, 8 * c["nh"]
            if tag == "G":
                e.lower_val(tagged("qk", "L", b, 2))
            wait_alone(e, at(c["src"][0], b, c["src"][1]))
            e.wait_ge(S[c["src"][0]], at(c["src"][0], b, c["src"][1]))
            if tag == "G":
                e.wait_ge(S["qk"], tagged("qk", "L", b, 2))
            bq, bk, bv = c["banks"]
            for k, bank in enumerate((bq, bk)):
                e.matmul(PS(bank)[0:mr, 0:n], c["w"][:, mr * k:mr * k + mr], c["xin"], start=True, stop=True).then_inc(S["qk_ps"], 1)
            for j in range(nt):
                last = e.matmul(PS(bv)[:, mr * j:mr * j + mr], c["xin"][:, P * j:P * j + P], c["w"][:, 2 * mr:3 * mr], start=(j == 0), stop=(j == nt - 1), skip_group_check=True)
            last.then_inc(S["v_ps"], 1)

        def pe_attn(e, b, tag, while_stacking=None, after_maxima=None):
            b = stage_turn(e, b)
            c = attn_shape(tag)
            QS, KS, vh = c["QS"], c["KS"], c["vh"]
            nh, n, nt, mr = c["nh"], c["n"], c["n"] // P, 8 * c["nh"]
            if tag != "G":
                pe_qkv(e, b, tag)
            if while_stacking:
                while_stacking(e, b)
            e.wait_ge(S["v"], tagged("v", tag, b, 1))
            if tag == "G":
                e.wait_ge(S["stacked_g"], at("stacked_g", b, 96))
            else:
                e.wait_ge(S["stacked"], tagged("stacked", tag, b, 96))
            if tag == "A":
                e.wait_ge(S["q_zero"], at("q_zero", b, 16))
            e.wait_ge(S["k_ones"], at("k_ones", b, 48 if tag == "A" else 32))
            for it, (hd, js) in enumerate(s1_items(c)):
                if it >= 3:
                    e.wait_ge(S["max"], tagged("max", tag, b, it - 2))
                for x, j in enumerate(js):
                    w = P * (j + 1) if c["causal"] else n
                    bank = PS(2 * (it % 3) + x)
                    last = e.matmul(bank[:, 0:w], QS[:, hd, P * j:P * j + P], KS[:, hd, 0:w], start=True, stop=not c["causal"])
                    if c["causal"]:
                        last = e.matmul(bank[:, P * j:P * j + P], identb[:, :], maskb[:, 0, :], start=False, stop=True)
                last.then_inc(S["s1"], 1)
            if after_maxima:
                after_maxima(e, b)
            wait_alone(e, tagged("nm", tag, b, 1))
            e.wait_ge(S["nm"], tagged("nm", tag, b, 1))
            for j in range(nt):
                last = e.transpose(PSB(6)[0:3 * nh, P * j:P * j + P], NM[:, j, 0:3 * nh], identb[:, :])
            last.then_inc(S["nm_t"], 1)
            e.wait_ge(S["nm_in"], tagged("nm_in", tag, b, 48))
            items = s2_items(c)

            def weighted(s):
                g, i, _ = items[2 * s]
                h, r = g // 2, g % 2
                e.wait_ge(S["p"], tagged("p", tag, b, 2 * s + 2))
                q0 = P * i if c["causal"] else 0
                for q in range(4):
                    last = e.matmul(PS(6 + h)[32 * q:32 * q + 32, q0:n], VP[:, i, vh + 8 * h + 2 * q + r, :],
                                    PT[:, (2 * s + q // 2) % 4, q % 2, q0:n], start=(r == 0 and i == 0), stop=(r == 1 and i == nt - 1), skip_group_check=True)
                last.then_inc(S["pv"], 1)

            for it, (g, i, pr) in enumerate(items):
                h, r = g // 2, g % 2
                if it >= 3:
                    e.wait_ge(S["p"], tagged("p", tag, b, it - 2))
                q0 = P * i if c["causal"] else 0
                for x in range(2):
                    hd = 8 * h + 2 * (2 * pr + x) + r
                    bank = PS(2 * (it % 3) + x)
                    last = e.matmul(bank[:, q0:n], KS[:, hd, P * i:P * i + P], QS[:, hd, q0:n], start=True, stop=not c["causal"])
                    if c["causal"]:
                        last = e.matmul(bank[:, q0:q0 + P], identb[:, :], maskb[:, 1, :], start=False, stop=True)
                last.then_inc(S["s2"], 1)
                if it % 2 == 1 and it >= 3:
                    weighted((it - 3) // 2)
            weighted(len(items) // 2 - 1)

        def act_qkv(e, b, tag):
            b = stage_turn(e, b)
            c = attn_shape(tag)
            nh, n, nt, mr = c["nh"], c["n"], c["n"] // P, 8 * c["nh"]
            if tag == "G":
                e.wait_ge(S["split"], tagged("split", "L", b, 1))
            for k in range(2):
                e.wait_ge(S["qk_ps"], tagged("qk_ps", tag, b, k + 1))
                e.activation(F[0:mr, k, 0:n], PS(c["banks"][k])[0:mr, 0:n], ACT.Identity, bias=bcol(c["bc"][k])[0:mr, :]).then_inc(S["qk"], 1)

        def act_attn(e, b, tag, while_stacking=None, after_maxima=None):
            b = stage_turn(e, b)
            c = attn_shape(tag)
            nh, n, nt, mr = c["nh"], c["n"], c["n"] // P, 8 * c["nh"]
            if tag != "G":
                act_qkv(e, b, tag)
            if while_stacking:
                while_stacking(e, b)
            if after_maxima:
                after_maxima(e, b)
            e.wait_ge(S["nm_t"], tagged("nm_t", tag, b, 1))
            e.activation(NMT[0:3 * nh, 0:n], PSB(6)[0:3 * nh, 0:n], ACT.Copy).then_inc(S["nmt"], 1)
            for it, (g, i, pr) in enumerate(s2_items(c)):
                q0 = P * i if c["causal"] else 0
                e.wait_ge(S["s2"], tagged("s2", tag, b, it + 1))
                if it >= 4:
                    e.wait_ge(S["pv"], tagged("pv", tag, b, it // 2 - 1))
                bk = 2 * (it % 3)
                e.activation(PT[:, it % 4, :, q0:n], PSall[:, bk:bk + 2, q0:n], ACT.Exp, scale=SCALE).then_inc(S["p"], 1)
            e.wait_ge(S["pv"], tagged("pv", tag, b, len(s2_items(c)) // 2))
            hh = nh // 8
            e.activation(OS[:, 0:hh, 0:n], PSall[:, 6:6 + hh, 0:n], ACT.Copy).then_inc(S["os"], 1)

        def dve_qkv(e, b, tag, step):
            b = stage_turn(e, b)
            c = attn_shape(tag)
            nh, n, nt, mr = c["nh"], c["n"], c["n"] // P, 8 * c["nh"]
            e.wait_ge(S["qk"], tagged("qk", tag, b, 2))
            f, part = F[0:mr, :, 0:n], lambda k: c["SPL"][0:mr, :, k, 0:n]
            step(e.tensor_copy(part(0), f))
            step(e.tensor_tensor(f, f, part(0), ALU.subtract))
            step(e.tensor_copy(part(1), f))
            e.tensor_tensor(part(2), f, part(1), ALU.subtract).then_inc(S["split"], 1)
            e.wait_ge(S["v_ps"], tagged("v_ps", tag, b, 1))
            for r in range(2):
                for j in range(nt):
                    v = VP[:, j, c["vh"]:c["vh"] + nh, :].rearrange("p (m r) c -> p m r c", r=2)[:, :, r, 16 * r:16 * r + 8]
                    ps = PS(c["banks"][2])[:, mr * j:mr * j + mr].rearrange("p (m r c) -> p m r c", r=2, c=HD)[:, :, r, :]
                    bv = c["bv"].rearrange("p (m r c) -> p m r c", r=2, c=HD)[:, :, r, :]
                    last = e.tensor_tensor(v, ps, bv, ALU.add)
            last.then_inc(S["v"], 1)

        def dve_attn(e, b, tag, step, while_stacking=None):
            b = stage_turn(e, b)
            c = attn_shape(tag)
            nh, n, nt, mr = c["nh"], c["n"], c["n"] // P, 8 * c["nh"]
            if tag != "G":
                dve_qkv(e, b, tag, step)
            if while_stacking:
                while_stacking(e, b)
            for it, (hd, js) in enumerate(s1_items(c)):
                e.wait_ge(S["s1"], tagged("s1", tag, b, it + 1))
                bk, w = 2 * (it % 3), P * (js[-1] + 1) if c["causal"] else n
                e.tensor_reduce(MX[:, js[0]:js[-1] + 1, hd], PSall[:, bk:bk + len(js), 0:w], AX.X, ALU.max).then_inc(S["max"], 1)
            e.wait_ge(S["max"], tagged("max", tag, b, len(s1_items(c))))
            f, part = NMF[:, 0:nt, 0:nh], lambda k: NM[:, 0:nt, nh * k:nh * k + nh]
            step(e.tensor_scalar(f, MX[:, 0:nt, 0:nh], -1.0, None, ALU.mult))
            step(e.tensor_copy(part(0), f))
            step(e.tensor_tensor(f, f, part(0), ALU.subtract))
            step(e.tensor_copy(part(1), f))
            e.tensor_tensor(part(2), f, part(1), ALU.subtract).then_inc(S["nm"], 1)
            if tag != "A":
                dve_heads_out(e, b, tag, nh // 8, n, step)

        def fill(e, stack, value, h0, h1, n):
            if n == P:
                return e.dma_start(stack[72:75, h0:h1, 0:P], ONEZ[:, value:value + 1, :].broadcast_to([3, h1 - h0, P]))
            dst = stack[72:75, h0:h1, :].rearrange("p n (j t) -> p (n j) t", j=NT)
            return e.dma_start(dst, ONEZ[:, value:value + 1, :].broadcast_to([3, (h1 - h0) * NT, P]))

        def sp_stack(e, b, tag):
            b = stage_turn(e, b)
            c = attn_shape(tag)
            nh, n, mr = c["nh"], c["n"], 8 * c["nh"]
            QS, KS, SPL, own = c["QS"], c["KS"], c["SPL"], "_g" if tag == "G" else ""
            q_out, k_out = ("split_out_g", "split_out_g") if tag == "G" else ("q_out", "k_out")
            if tag == "A":
                e.wait_ge(S["pv"], tagged("pv", tag, b, 0))
                fill(e, QS, 0, 0, nh, n).then_inc(S["q_zero"], 16)
            e.wait_ge(S["split"], tagged("split", tag, b, 1))
            for k in range(3):
                dst = bass.AP(c["qd"].tensor, k * HD * T, [[3 * HD * T, nh], [T, HD], [1, n]])
                e.dma_start(dst, SPL[0:mr, 0, k, 0:n]).then_inc(S[q_out], 16)
            for k in range(5):
                dst = bass.AP(c["kd"].tensor, k * HD * T, [[5 * HD * T, nh], [T, HD], [1, n]])
                e.dma_start(dst, SPL[0:mr, 1, KTYPES[k], 0:n]).then_inc(S[k_out], 16)
            e.wait_ge(S[q_out], at(q_out, b, 128) if tag == "G" else tagged(q_out, tag, b, 48))
            for r in range(3):
                e.dma_start(QS[24 * r:24 * r + 24, 0:nh, 0:n], bass.AP(c["qd"].tensor, 0, [[T, 24], [3 * HD * T, nh], [1, n]])).then_inc(S[f"stacked{own}"], 16)
            e.wait_ge(S[k_out], at(k_out, b, 128) if tag == "G" else tagged(k_out, tag, b, 80))
            for r in range(3):
                e.dma_start(KS[24 * r:24 * r + 24, 0:nh, 0:n], bass.AP(c["kd"].tensor, r * HD * T, [[T, 24], [5 * HD * T, nh], [1, n]])).then_inc(S[f"stacked{own}"], 16)

        def sp_maxima(e, b, tag):
            b = stage_turn(e, b)
            c = attn_shape(tag)
            nh, n = c["nh"], c["n"]
            e.wait_ge(S["nmt"], tagged("nmt", tag, b, 1))
            for r in range(3):
                e.dma_start(c["QS"][72 + r:73 + r, 0:nh, 0:n], NMT[nh * r:nh * r + nh, 0:n]).then_inc(S["nm_in"], 16)

        def pool_l1(e, b):
            b = stage_turn(e, b)
            wait_alone(e, at("band_used", b, 4))
            e.wait_ge(S["band_used"], at("band_used", b, 4))
            e.memset(U[:, 0:NH * T].rearrange("p (k s) -> p k s", k=4)[:, 0::2, :], 0.0).then_inc(S["stack_zero"], 1)
            e.memset(QSG, 0.0).then_inc(S["stack_zero"], 1)
            e.memset(KSG, 0.0).then_inc(S["stack_zero"], 1)

        def pool_l3(e, b):
            b = stage_turn(e, b)
            wait_alone(e, at("w1_used", b, E1))
            e.wait_ge(S["w1_used"], at("w1_used", b, E1))
            e.memset(U[:, 0:NH * T].rearrange("p (k s) -> p k s", k=4)[:, 1::2, :], 0.0).then_inc(S["stack_zero"], 1)

        def sp_l1(e, b):
            b = stage_turn(e, b)
            e.wait_ge(S["stack_zero"], at("stack_zero", b, 3))
            fill(e, KS, 1, 0, 8, T).then_inc(S["k_ones"], 16)
            fill(e, KSG, 1, 0, 8, P).then_inc(S["k_ones"], 16)
            sp_stack(e, b, "L")
            sp_stack(e, b, "G")
            for x in range(WSLOTS):
                sp_w1(e, b, x)
            sp_maxima(e, b, "L")
            sp_maxima(e, b, "G")

        def pe_early1(e, b):
            for r in range(R1):
                last = e.matmul(PS(7)[0:LD, 0:P], wcomp[:, r, :], XT[:, :].rearrange("p (t r) -> p t r", r=R1)[:, :, r], start=(r == 0), stop=(r == R1 - 1))
            last.then_inc(S["cg_ps"], 1)
            for f in range(NF):
                e.matmul(PS(3 + f), rw1[:, P * f:P * f + P], XT[:, :], start=True, stop=True).then_inc(S["r_ps"], 1)
            pe_qkv(e, b, "G")
            e.wait_ge(S["qk"], tagged("qk", "G", b, 1))
            for f in range(NF):
                e.wait_ge(S["r"], at("r", b, f + 1))
                last = e.matmul(PS(7)[0:E1, :], rw2[:, f, :], HB[:, 1, f, :], start=(f == 0), stop=(f == NF - 1))
            last.then_inc(S["f1_ps"], 1)
            wait_alone(e, at("sc1", b, 1))
            e.wait_ge(S["sc1"], at("sc1", b, 1))
            for j in range(NT):
                last = e.transpose(PS(3)[:, E1 * j:E1 * j + E1], SC8[:, P * j:P * j + P], ident[0:E1, 0:E1])
            last.then_inc(S["f1_ps"], 1)

        def act_early1(e, b):
            e.wait_ge(S["cg_ps"], at("cg_ps", b, 1))
            e.activation(CGT[:, :], PS(7)[0:LD, 0:P], ACT.Identity, bias=bcol(44)[0:LD, :]).then_inc(S["cgt"], 1)
            for f in range(NF):
                e.wait_ge(S["r_ps"], at("r_ps", b, f + 1))
                e.activation(HB[:, 1, f, :], PS(3 + f), ACT.Relu, bias=bcol(32 + f)).then_inc(S["r"], 1)
            act_qkv(e, b, "G")
            e.wait_ge(S["f1_ps"], at("f1_ps", b, 1))
            e.activation(SC8, PS(7)[0:E1, :], ACT.Identity, bias=rb2[:, :]).then_inc(S["sc1"], 1)
            act_topk(e, b, "g1", P, NT, E1)

        def dve_early1(e, b, step):
            dve_qkv(e, b, "G", step)
            e.wait_ge(S["f1_ps"], at("f1_ps", b, 2))
            step(e.tensor_copy(SCO[:, :, 0:E1], PS(3)[:, 0:NT * E1].rearrange("p (j n) -> p j n", j=NT)), alone=True)
            dve_topk(e, b, "g1", P, NT, E1, 2, step)
            e.tensor_copy(DIF[:, :, 0:E1], GT[:, :, 0:E1]).then_inc(S["g1"], 1)

        def pe_l1(e, b):
            b = stage_turn(e, b)
            pe_attn(e, b, "L", pe_early1)
            pe_heads_out(e, b, "L", 1, T, WLGP[:, 0:1, :], PS(0), LD)
            e.wait_ge(S["lo"], at("lo", b, 1))
            pe_attn(e, b, "G")
            pe_heads_out(e, b, "G", 1, P, WLGP[:, 1:2, :], PS(0), LD)
            e.wait_ge(S["go"], at("go", b, 1))
            for j in range(NT):
                last = e.matmul(PS(1)[:, LD * j:LD * j + LD], cn("expand4")[:, P * j:P * j + P], GO[:, :], start=(j == 0), stop=(j == NT - 1), skip_group_check=True)
            last.then_inc(S["go_all"], 1)

        def act_l1(e, b):
            b = stage_turn(e, b)
            act_attn(e, b, "L", act_early1)
            act_attn(e, b, "G")
            e.wait_ge(S["mix_dif"], at("mix_dif", b, 1))
            e.activation(PR[:, :, 1], PR[:, :, 0], ACT.Tanh, scale=0.5).then_inc(S["mix_tanh"], 1)

        def dve_l1(e, b, step):
            b = stage_turn(e, b)
            dve_attn(e, b, "L", step, lambda e, b: dve_early1(e, b, step))
            e.wait_ge(S["proj"], tagged("proj", "L", b, 1))
            e.tensor_tensor(LO[:, :, 0:LD], PS(0)[:, 0:NT * LD].rearrange("p (j c) -> p j c", j=NT), rc["b_lproj"].unsqueeze(1).broadcast_to([P, NT, LD]), ALU.add).then_inc(S["lo"], 1)
            dve_attn(e, b, "G", step)
            e.wait_ge(S["proj"], tagged("proj", "G", b, 1))
            e.tensor_tensor(GO[:, :], PS(0)[:, 0:LD], rc["b_gproj"], ALU.add).then_inc(S["go"], 1)
            e.wait_ge(S["go_all"], at("go_all", b, 1))
            e.tensor_copy(LO[:, :, LD:C], PS(1)[:, 0:NT * LD].rearrange("p (j c) -> p j c", j=NT)).then_inc(S["go_seen"], 1)
            e.wait_ge(S["go_seen"], at("go_seen", b, 1))
            step(e.tensor_tensor(SB[:, :, :], LO[:, :, :], WDIF[:, 0:C].unsqueeze(1).broadcast_to([P, NT, C]), ALU.mult))
            step(e.tensor_reduce(SM[:, :], SB[:, :, :], AX.X, ALU.add))
            e.tensor_scalar(PR[:, :, 0], SM[:, :], WDIF[:, C:C + 1], None, ALU.add).then_inc(S["mix_dif"], 1)
            e.wait_ge(S["mix_tanh"], at("mix_tanh", b, 1))
            step(e.tensor_scalar(PR[:, :, 0], PR[:, :, 1], 0.5, 0.5, ALU.mult, ALU.add))
            step(e.tensor_scalar(PR[:, :, 1], PR[:, :, 1], -0.5, 0.5, ALU.mult, ALU.add))
            for k in range(2):
                last = e.tensor_tensor(SB[:, :, LD * k:LD * k + LD], LO[:, :, LD * k:LD * k + LD], PR[:, :, k:k + 1].broadcast_to([P, NT, LD]), ALU.mult)
            step(last)

        def sp_w1(e, b, x):
            b = stage_turn(e, b)
            e.dma_start(wslot[x % WSLOTS][:, 0, :], a["L1_ffn_W1"][x]).then_inc(S[f"w1_in{x % WSLOTS}"], 16)
            e.dma_start(wslot[x % WSLOTS][:, 1, :].rearrange("p (f c) -> p f c", f=NF), a["L1_ffn_W2"][x].rearrange("(f p) c -> p f c", p=P)).then_inc(S[f"w1_in{x % WSLOTS}"], 16)

        def sp_f1(e, b):
            b = stage_turn(e, b)
            for x in range(WSLOTS, E1):
                e.wait_ge(S["w1_used"], at("w1_used", b, x - WSLOTS + 1))
                sp_w1(e, b, x)

        def pe_f1(e, b):
            b = stage_turn(e, b)
            e.wait_ge(S["go_seen"], at("go_seen", b, 1))

            def up(x):
                e.wait_ge(S[f"w1_in{x % WSLOTS}"], at(f"w1_in{x % WSLOTS}", b, 32 * (x // WSLOTS) + 32))
                for f in range(NF):
                    if x > 0:
                        e.wait_ge(S["h1"], at("h1", b, NF * (x - 1) + f + 1))
                    e.matmul(PS(f), wslot[x % WSLOTS][:, 0, P * f:P * f + P], XT[:, :], start=True, stop=True).then_inc(S["h1_ps"], 1)

            def down(x):
                if x >= 2:
                    e.wait_ge(S["acc1"], at("acc1", b, x - 1))
                e.wait_ge(S["h1"], at("h1", b, NF * x + NF))
                for j in range(NT):
                    for f in range(NF):
                        last = e.matmul(PS(6 + x % 2)[:, P * j:P * j + P], HB[:, x % 2, f, P * j:P * j + P], wslot[x % WSLOTS][:, 1, P * f:P * f + P],
                                        start=(j == 0 and f == 0), stop=(j == NT - 1 and f == NF - 1), skip_group_check=True)
                last.then_inc(S["w1_used"], 1)

            up(0)
            e.wait_ge(S["g1"], at("g1", b, 1))
            for j in range(NT):
                last = e.transpose(PS(4)[0:E1, P * j:P * j + P], GT[:, j, 0:E1], ident)
            last.then_inc(S["f1_ps"], 1)
            e.wait_ge(S["g1_row"], at("g1_row", b, 1))
            for j in range(NT):
                last = e.matmul(PS(5)[:, P * j:P * j + P], SCT[:, P * j:P * j + P], b2[:, :], start=(j == 0), stop=(j == NT - 1), skip_group_check=True)
            last.then_inc(S["f1_ps"], 1)
            for x in range(1, E1):
                up(x)
                down(x - 1)
            down(E1 - 1)

        def act_f1(e, b):
            b = stage_turn(e, b)
            for x in range(E1):
                for f in range(NF):
                    e.wait_ge(S["h1_ps"], at("h1_ps", b, NF * x + f + 1))
                    if x >= 2 and f == 0:
                        e.wait_ge(S["w1_used"], at("w1_used", b, x - 1))
                    e.activation(HB[:, x % 2, f, :], PS(f), ACT.Relu, bias=bcol(NF * x + f)).then_inc(S["h1"], 1)
                if x == 0:
                    e.wait_ge(S["f1_ps"], at("f1_ps", b, 3))
                    e.activation(SCT[:, :], PS(4)[0:E1, :], ACT.Copy).then_inc(S["g1_row"], 1)
            act_gate(e, b, 1)

        def dve_f1(e, b, step):
            b = stage_turn(e, b)
            e.wait_ge(S["f1_ps"], at("f1_ps", b, 4))
            step(e.tensor_copy(GB[:, :, :], PS(5).rearrange("p (j c) -> p j c", j=NT)))
            for x in range(E1):
                e.wait_ge(S["w1_used"], at("w1_used", b, x + 1))
                for j in range(NT):
                    last = e.scalar_tensor_tensor(out=GB[:, j, :], in0=PS(6 + x % 2)[:, P * j:P * j + P], scalar=GT[:, j, x:x + 1], in1=GB[:, j, :], op0=ALU.mult, op1=ALU.add)
                last.then_inc(S["acc1"] if x < E1 - 1 else S["f"], 1)
                if x < E1 - 1:
                    e.wait_ge(S["acc1"], at("acc1", b, x + 1))
                else:
                    e.wait_ge(S["f"], at("f", b, 2))
            dve_update(e, b, 1, step)

        EPS2 = 1e-6

        def pe_l2(e, b):
            b = stage_turn(e, b)
            e.wait_ge(S["xt"], at("xt", b, 3))
            e.matmul(PS(1), WT[:, T_QKV, :], XT[:, :], start=True, stop=True).then_inc(S["l2_ps"], 1)
            kv_w = WT[:, T_QKV + 1:T_QKV + 3, :].rearrange("p a c -> p (a c)")
            for j in range(NT):
                last = e.matmul(PS(2 + j // 2)[:, 256 * (j % 2):256 * (j % 2) + 256], XT[:, P * j:P * j + P], kv_w, start=(j % 2 == 0), stop=(j % 2 == 1), skip_group_check=True)
            last.then_inc(S["l2_ps"], 1)
            e.wait_ge(S["l2_sb"], at("l2_sb", b, 1))
            for j in range(NT):
                e.matmul(PS(4)[:, 0:C], KV[:, j, 1, :], KV[:, j, 0, :], start=(j == 0), stop=(j == NT - 1))
                last = e.matmul(PS(5)[:, 0:1], KV[:, j, 0, :], one1[:, :], start=(j == 0), stop=(j == NT - 1))
            last.then_inc(S["l2_ps"], 1)
            e.wait_ge(S["l2_sb"], at("l2_sb", b, 3))
            e.matmul(PS(6)[:, 0:C], KVT[:, :], WT[:, T_WO2, :], start=True, stop=True).then_inc(S["l2_ps"], 1)
            e.wait_ge(S["l2_sb"], at("l2_sb", b, 4))
            e.wait_ge(S["l2_sb"], at("l2_sb", b, 2))
            for j in range(NT):
                last = e.matmul(PS(2 + j // 2)[:, 256 * (j % 2):256 * (j % 2) + C + 1], HT[:, P * j:P * j + P], KVO[:, :], start=(j % 2 == 0), stop=(j % 2 == 1), skip_group_check=True)
            last.then_inc(S["l2_ps"], 1)

        def dve_l2(e, b, step):
            b = stage_turn(e, b)
            e.wait_ge(S["l2_ps"], at("l2_ps", b, 2))
            ps = PSall[:, 2:4, :].rearrange("p a (j s c) -> p (a j) s c", j=2, s=2)
            step(e.tensor_scalar(KV[:, :, 0, :], ps[:, :, 0, :], 0.0, EPS2, ALU.max, ALU.add))
            e.tensor_copy(KV[:, :, 1, :], ps[:, :, 1, :]).then_inc(S["l2_sb"], 1)
            e.wait_ge(S["l2_ps"], at("l2_ps", b, 1))
            e.tensor_scalar(HT[:, :], PS(1), 0.0, EPS2, ALU.max, ALU.add).then_inc(S["l2_sb"], 1)
            e.wait_ge(S["l2_ps"], at("l2_ps", b, 3))
            e.tensor_copy(KVO[:, C:C + 1], PS(5)[:, 0:1])
            e.tensor_copy(KVT[:, :], PS(4)[:, 0:C]).then_inc(S["l2_sb"], 1)
            e.wait_ge(S["l2_ps"], at("l2_ps", b, 4))
            e.tensor_copy(KVO[:, 0:C], PS(6)[:, 0:C]).then_inc(S["l2_sb"], 1)
            e.wait_ge(S["l2_ps"], at("l2_ps", b, 5))
            o = PSall[:, 2:4, :].rearrange("p a (j c) -> p (a j) c", j=2)
            step(e.tensor_scalar(SM[:, :], o[:, :, C], EPS2, None, ALU.add))
            step(e.reciprocal(SM[:, :], SM[:, :]))
            for j in range(NT):
                last = e.scalar_tensor_tensor(out=SB[:, j, :], in0=o[:, j, 0:C], scalar=SM[:, j:j + 1], in1=rc["b_out"], op0=ALU.mult, op1=ALU.add)
            last.then_inc(S["o2"], 1)
            e.wait_ge(S["o2"], at("o2", b, 1))

        def ffn_shape(l):
            if l == 2:
                return dict(npair=E2 // 2, ne=E2,
                            up=lambda p: (WT[:, T_W1 + p, :], WT[:, T_W3 + p, :]), down=lambda p: WT[:, T_W2 + p, :],
                            shared=(WT[:, T_SW13, 0:64], WT[:, T_SW13, 64:128], WT[0:64, T_SW2, :]),
                            gate=WT[:, T_GATES, 8:24])
            return dict(npair=E3 // 2, ne=E3,
                        up=lambda p: (WG3[:, 2 * p:2 * p + 2, :].rearrange("p e f -> p (e f)"), WU3[:, 2 * p:2 * p + 2, :].rearrange("p e f -> p (e f)")),
                        down=lambda p: WD3[:, p, :], shared=(WS3[:, 0, :], WS3[:, 1, :], WSD3[:, :]), gate=WT[:, T_GATES, 24:88])

        def pe_scores(e, b, l):
            c = ffn_shape(l)
            ne = c["ne"]
            for j in range(NT):
                last = e.matmul(PS(7)[:, ne * j:ne * j + ne], XT[:, P * j:P * j + P], c["gate"], start=(j == 0), stop=(j == NT - 1), skip_group_check=True)
            last.then_inc(S["sc_ps"], 1)

        def pe_combine(e, b, l):
            wait_alone(e, paired("cb", l, b, 1))
            e.wait_ge(S["cb"], paired("cb", l, b, 1))
            for j in range(NT):
                if l == 2:
                    last = e.transpose(PSB(7)[0:48, P * j:P * j + P], CB[:, j, 0:48], identb[:, :])
                else:
                    e.transpose(PSB(7)[:, P * j:P * j + P], CB[:, j, 0:128], identb[:, :])
                    last = e.transpose(PSB(7)[0:64, T + P * j:T + P * j + P], CB[:, j, 128:192], identb[:, :])
            last.then_inc(S["ct_ps"], 1)

        def den3(e, b, h):
            e.wait_ge(S["os"], tagged("os", "A", b, 1))
            e.matmul(PS(7), cn("sel_den"), OS[:, h, :], start=True, stop=True).then_inc(S["den3"], 1)

        def pe_pairs(e, b, l):
            b = stage_turn(e, b)
            c = ffn_shape(l)
            npair, ne = c["npair"], c["ne"]
            if l == 2:
                e.wait_ge(S["o2"], at("o2", b, 1))
                pe_scores(e, b, 2)
            else:
                den3(e, b, 0)

            def up(p):
                k = 3 * (p % 2)
                m = P if p < npair else 64
                w1, w3 = c["up"](p) if p < npair else c["shared"][0:2]
                if p >= 2:
                    e.wait_ge(S["av"], paired("av", l, b, p - 1))
                e.matmul(PS(k)[0:m, :], w1, XT[:, :], start=True, stop=True).then_inc(S["u_ps"], 1)
                e.matmul(PS(k + 1)[0:m, :], w3, XT[:, :], start=True, stop=True)
                if p == 0:
                    if l == 2:
                        pe_combine(e, b, 2)
                    wait_alone(e, paired("ct", l, b, 1))
                    e.wait_ge(S["ct"], paired("ct", l, b, 1))
                if p < npair:
                    for x in range(2):
                        o = PS(k + 2)[64 * x:64 * x + 64, :]
                        ex = 2 * p + x
                        if l == 2:
                            last = e.matmul(o, hot16b[:, ex:ex + 1].broadcast_to([48, 64]), CT[0:48, 0, :], start=True, stop=True)
                        else:
                            e.matmul(o, hot64b[:, ex:ex + 1].broadcast_to([P, 64]), CT[:, 0, :], start=True, stop=False)
                            last = e.matmul(o, hot64b[0:64, ex:ex + 1].broadcast_to([64, 64]), CT[0:64, 1, :], start=False, stop=True)
                    last.then_inc(S["w_ps"], 1)
                else:
                    e.matmul(PS(k + 2)[0:1, 0:1], one1[0:1, :], one1[0:1, :], start=True, stop=True).then_inc(S["w_ps"], 1)

            def down(p):
                m = P if p < npair else 64
                w = c["down"](p) if p < npair else c["shared"][2]
                e.wait_ge(S["av"], paired("av", l, b, p + 1))
                for j in range(NT):
                    last = e.matmul(PS(6)[:, P * j:P * j + P], AV[0:m, p % 2, P * j:P * j + P], w,
                                    start=(p == 0 and j == 0), stop=(p == npair and j == NT - 1), skip_group_check=True)
                last.then_inc(S["down"], 1)

            if l == 3:
                e.wait_ge(S["w_late"], loaded["w_late"])
            up(0)
            for p in range(1, npair + 1):
                if l == 3 and p == 3:
                    e.wait_ge(S["rc3"], at("rc3", b, 1))
                    den3(e, b, 1)
                if l == 3 and p == 8:
                    e.wait_ge(S["sq3"], at("sq3", b, 1))
                    for h in range(2):
                        last = e.matmul(PS(7)[32 * h:32 * h + 8, :], cn("sum_group"), RC[:, h, :], start=True, stop=True)
                    last.then_inc(S["n3_ps"], 1)
                up(p)
                down(p - 1)
            down(npair)

        def act_sig3(e, b):
            e.wait_ge(S["sc_ps"], paired("sc_ps", 3, b, 1))
            e.activation(SCO[:, :, :], PS(7)[:, 0:NT * E3].rearrange("p (j n) -> p j n", j=NT), ACT.Tanh, scale=0.5).then_inc(S["sig3"], 1)

        def act_combine(e, b, l):
            e.wait_ge(S["ct_ps"], paired("ct_ps", l, b, 1))
            if l == 2:
                e.activation(CT[0:48, 0, :], PSB(7)[0:48, 0:T], ACT.Copy).then_inc(S["ct"], 1)
            else:
                e.activation(CT[:, 0, :], PSB(7)[:, 0:T], ACT.Copy)
                e.activation(CT[0:64, 1, :], PSB(7)[0:64, T:2 * T], ACT.Copy).then_inc(S["ct"], 1)

        def act_pairs(e, b, l):
            b = stage_turn(e, b)
            c = ffn_shape(l)
            if l == 2:
                act_topk(e, b, "g2", P, NT, E2)
                act_combine(e, b, 2)
            for p in range(c["npair"] + 1):
                m = P if p < c["npair"] else 64
                e.wait_ge(S["u_ps"], paired("u_ps", l, b, p + 1))
                if p >= 2:
                    e.wait_ge(S["av"], paired("av", l, b, p - 1))
                e.activation(SL[0:m, p % 2, :], PS(3 * (p % 2))[0:m, :], ACT.Silu).then_inc(S["sl"], 1)
            act_gate(e, b, l)

        def dve_combine(e, b, l, step):
            ne = ffn_shape(l)["ne"]
            g, part = GT[:, :, 0:ne], lambda k: CB[:, :, ne * k:ne * k + ne]
            step(e.tensor_copy(part(0), g))
            step(e.tensor_tensor(g, g, part(0), ALU.subtract))
            step(e.tensor_copy(part(1), g))
            e.tensor_tensor(part(2), g, part(1), ALU.subtract).then_inc(S["cb"], 1)

        def dve_pairs(e, b, l, step):
            b = stage_turn(e, b)
            c = ffn_shape(l)
            npair, ne = c["npair"], c["ne"]
            if l == 2:
                e.wait_ge(S["sc_ps"], paired("sc_ps", 2, b, 1))
                step(e.tensor_copy(SCO[:, :, 0:ne], PS(7)[:, 0:NT * ne].rearrange("p (j n) -> p j n", j=NT)), alone=True)
                dve_topk(e, b, "g2", P, NT, ne, K2, step)
                dve_combine(e, b, 2, step)
            for p in range(npair + 1):
                k = 3 * (p % 2)
                m = P if p < npair else 64
                if l == 3 and p in (1, 4):
                    h = p // 4
                    e.wait_ge(S["den3"], at("den3", b, h + 1))
                    e.reciprocal(RC[:, h, :], PS(7)).then_inc(S["rc3"], 1)
                if l == 3 and p == 6:
                    e.wait_ge(S["rc3"], at("rc3", b, 2))
                    e.tensor_tensor(OS[:, :, :], OS[:, :, :], RC, ALU.mult).then_inc(S["on"], 1)
                    e.wait_ge(S["on"], tagged("on", "A", b, 1))
                    e.tensor_tensor(RC, OS[:, :, :], OS[:, :, :], ALU.mult).then_inc(S["sq3"], 1)
                if l == 3 and p == 10:
                    e.wait_ge(S["n3_ps"], at("n3_ps", b, 1))
                    for h in range(2):
                        last = e.tensor_copy(F[32 * h:32 * h + 8, 0, :], PS(7)[32 * h:32 * h + 8, :])
                    last.then_inc(S["s3"], 1)
                e.wait_ge(S["sl"], paired("sl", l, b, p + 1))
                e.wait_ge(S["w_ps"], paired("w_ps", l, b, p + 1))
                if p >= 2:
                    e.wait_ge(S["down"], paired("down", l, b, p - 1))
                if p < npair:
                    step(e.tensor_tensor(SL[:, p % 2, :], SL[:, p % 2, :], PS(k + 1), ALU.mult))
                    e.tensor_tensor(AV[:, p % 2, :], SL[:, p % 2, :], PS(k + 2), ALU.mult).then_inc(S["av"], 1)
                else:
                    e.tensor_tensor(AV[0:m, p % 2, :], SL[0:m, p % 2, :], PS(k + 1)[0:m, :], ALU.mult).then_inc(S["av"], 1)
            e.wait_ge(S["down"], paired("down", l, b, npair + 1))
            e.tensor_copy(GB[:, :, :], PS(6).rearrange("p (j c) -> p j c", j=NT)).then_inc(S["f"], 1)

        def dve_gate3(e, b, step):
            b = stage_turn(e, b)
            e.wait_ge(S["sig3"], at("sig3", b, 1))
            step(e.tensor_scalar(SCO[:, :, :], SCO[:, :, :], 0.5, 0.5, ALU.mult, ALU.add))
            step(e.tensor_tensor(DIF[:, :, :], SCO[:, :, :], rc["gate_bias"].unsqueeze(1).broadcast_to([P, NT, E3]), ALU.add), alone=True)
            for j in range(NT):
                for g in range(G3):
                    last = e.max(MG[:, j, g, :], DIF[:, j, 8 * g:8 * g + 8])
            step(last)
            step(e.tensor_tensor(GS[:, :, :], MG[:, :, :, 0], MG[:, :, :, 1], ALU.add), alone=True)
            for j in range(NT):
                last = e.max(M8[:, j, :], GS[:, j, :])
            step(last)
            step(e.memset(M8[:, :, TG3:8], GONE), alone=True)
            for j in range(NT):
                last = e.match_replace(GM[:, j, :], M8[:, j, :], GS[:, j, :], GONE)
            step(last)
            step(e.tensor_scalar(GM[:, :, :], GM[:, :, :], GONE / 2, None, ALU.is_le))
            step(e.tensor_scalar(GM[:, :, :], GM[:, :, :], -NEG, NEG, ALU.mult, ALU.add))
            for j in range(NT):
                last = e.tensor_tensor(DIF[:, j, :].rearrange("p (g n) -> p g n", g=G3), DIF[:, j, :].rearrange("p (g n) -> p g n", g=G3), GM[:, j, :].unsqueeze(2).broadcast_to([P, G3, 8]), ALU.add)
            step(last, alone=True)
            for j in range(NT):
                last = e.max(M8[:, j, :], DIF[:, j, :])
            step(last, alone=True)
            for j in range(NT):
                last = e.match_replace(RPL[:, j, :], M8[:, j, :], DIF[:, j, :], GONE)
            step(last)
            step(e.tensor_scalar(MSK[:, :, :], RPL[:, :, :], GONE / 2, None, ALU.is_le))
            step(e.tensor_tensor(GT[:, :, :], SCO[:, :, :], MSK[:, :, :], ALU.mult))
            step(e.tensor_reduce(SM[:, :], GT[:, :, :], AX.X, ALU.add))
            step(e.tensor_scalar(SM[:, :], SM[:, :], 1e-20, None, ALU.add))
            step(e.reciprocal(SM[:, :], SM[:, :]))
            step(e.tensor_scalar(SM[:, :], SM[:, :], HI3, None, ALU.mult))
            step(e.tensor_tensor(GT[:, :, :], GT[:, :, :], SM[:, :].unsqueeze(2).broadcast_to([P, NT, E3]), ALU.mult))

        def pe_l3(e, b):
            b = stage_turn(e, b)
            pe_attn(e, b, "A", lambda e, b: pe_scores(e, b, 3), lambda e, b: pe_combine(e, b, 3))

        def dve_l3(e, b, step):
            b = stage_turn(e, b)
            def gate(e, b):
                dve_gate3(e, b, step)
                dve_combine(e, b, 3, step)

            dve_attn(e, b, "A", step, gate)

        def sp_l3(e, b):
            b = stage_turn(e, b)
            e.wait_ge(S["stack_zero"], at("stack_zero", b, 4))
            fill(e, KS, 1, 8, 16, T).then_inc(S["k_ones"], 16)
            sp_stack(e, b, "A")
            sp_maxima(e, b, "A")
            wait_alone(e, tagged("on", "A", b, 1))
            e.wait_ge(S["on"], tagged("on", "A", b, 1))
            e.dma_start(o_dram[b], OS[:, :, :]).then_inc(S["o_saved"], 16)
            wait_alone(e, at("s3", b, 1))
            e.wait_ge(S["s3"], at("s3", b, 1))
            for h in range(2):
                e.dma_start(n_dram[h, :, b, :], F[32 * h:32 * h + 8, 0, :]).then_inc(S["n_saved"], 16)


        N2 = D[0:16, 0:B * T].rearrange("p (b t) -> p b t", b=B)
        O3 = [U[:, 1024 * i:1024 * i + 1024].rearrange("p (h t) -> p h t", h=2) for i in range(2)]
        X3 = [U[:, 2048 + 512 * i:2560 + 512 * i].rearrange("p (j c) -> p j c", j=NT) for i in range(2)]
        G3B = [U[:, 3072 + 512 * i:3584 + 512 * i].rearrange("p (j c) -> p j c", j=NT) for i in range(2)]
        Y3 = [U[:, 4096 + 512 * i:4608 + 512 * i].rearrange("p (j c) -> p j c", j=NT) for i in range(2)]
        FC = sb("FC", [16, 8])
        BO = XN[0:16, 1, :]
        BOR = XN[:, 0, :]
        WFC = sb("WFC", [P, 2])
        WOF = SB[:, 0:2, :]

        def sp_final(e):
            e.dma_start(BO[:, :], a["L3_attn_bo"]).then_inc(S["fin_w"], 16)
            e.dma_start(FC[:, 3:4], a["L3_attn_gate"].rearrange("(h o) -> h o", o=1)).then_inc(S["fin_w"], 16)
            for s in ("n_saved", "o_saved", "x_saved", "g_saved"):
                e.wait_ge(S[s], at(s, B, 0))
            e.dma_start(N2, n_dram.rearrange("h g b t -> (h g) b t")).then_inc(S["fin_n"], 16)
            with e.Fori(0, B // 2) as i:
                for k in range(2):
                    e.dma_start(O3[k], o_dram[2 * i + k]).then_inc(S[f"fin_in{k}"], 16)
                    e.dma_start(X3[k], x_dram[2 * i + k]).then_inc(S[f"fin_in{k}"], 16)
                    e.dma_start(G3B[k], g_dram[2 * i + k]).then_inc(S[f"fin_in{k}"], 16)
                for k in range(2):
                    e.wait_ge(S[f"fin_used{k}"], i + 1)
                    e.dma_start(out[2 * i + k].rearrange("(j p) c -> p j c", p=P), Y3[k]).then_inc(S[f"fin_out{k}"], 16)
                wait_alone(e, 16 * i + 16)
                for k in range(2):
                    e.wait_ge(S[f"fin_out{k}"], 16 * i + 16)
            for k in range(2):
                e.wait_ge(S[f"fin_out{k}"], 16 * (B // 2))

        def act_final(e):
            e.wait_ge(S["fin_n"], 16)
            e.activation(N2, N2, ACT.Sqrt, accum_out=FC[:, 0:1]).then_inc(S["fin_sqrt"], 1)

        def dve_final(e):
            n = [0]

            def step(ins):
                n[0] += 1
                ins.then_inc(S["fin_dve"], 1)
                e.wait_ge(S["fin_dve"], n[0])

            e.wait_ge(S["fin_sqrt"], 1)
            e.wait_ge(S["fin_w"], 32)
            step(e.tensor_scalar(FC[:, 1:2], FC[:, 0:1], 1.0 / (B * T), 1e-5, ALU.mult, ALU.max))
            step(e.reciprocal(FC[:, 2:3], FC[:, 1:2]))
            step(e.tensor_scalar(FC[:, 3:4], FC[:, 3:4], 0.0, 1.0, ALU.max, ALU.min))
            step(e.tensor_scalar(FC[:, 4:5], FC[:, 3:4], 1.0 / NH, None, ALU.mult))
            e.tensor_tensor(FC[:, 5:6], FC[:, 4:5], FC[:, 2:3], ALU.mult).then_inc(S["fin_fac"], 1)
            e.wait_ge(S["fin_mm"], 1)
            step(e.tensor_copy(WFC[:, :], PS(0)[:, 0:2]))
            for h in range(2):
                e.tensor_scalar(WOF[:, h, :], WOP[:, h, :], WFC[:, h:h + 1], None, ALU.mult)
            e.tensor_copy(BOR[:, :], PS(1)[:, 0:C]).then_inc(S["fin_w2"], 1)
            e.wait_ge(S["fin_w2"], 1)
            with e.Fori(0, B // 2) as i:
                for k in range(2):
                    e.wait_ge(S[f"fin_in{k}"], 48 * i + 48)
                    e.wait_ge(S["fin_y"], 2 * i + k + 1)
                    e.tensor_tensor(Y3[k], PS(2 + k).rearrange("p (j c) -> p j c", j=NT), BOR[:, :].unsqueeze(1).broadcast_to([P, NT, C]), ALU.add).then_inc(S["fin_c"], 1)
                    e.wait_ge(S["fin_c"], 4 * i + 2 * k + 1)
                    e.tensor_tensor(Y3[k], Y3[k], G3B[k], ALU.mult).then_inc(S["fin_c"], 1)
                    e.wait_ge(S["fin_c"], 4 * i + 2 * k + 2)
                    e.tensor_tensor(Y3[k], Y3[k], X3[k], ALU.add).then_inc(S[f"fin_used{k}"], 1)

        def pe_final(e):
            e.wait_ge(S["fin_fac"], 1)
            for h in range(2):
                e.matmul(PS(0)[:, h:h + 1], cn(f"head_row{h}")[0:16, :], FC[:, 5:6], start=(h == 0), stop=(h == 1), skip_group_check=True)
            e.matmul(PS(1)[:, 0:C], FC[:, 4:5].broadcast_to([16, P]), BO[:, :], start=True, stop=True).then_inc(S["fin_mm"], 1)
            e.wait_ge(S["fin_w2"], 1)
            with e.Fori(0, B // 2) as i:
                for k in range(2):
                    e.wait_ge(S[f"fin_in{k}"], 48 * i + 48)
                    for j in range(NT):
                        for h in range(2):
                            last = e.matmul(PS(2 + k)[:, P * j:P * j + P], O3[k][:, h, P * j:P * j + P], WOF[:, h, :],
                                            start=(j == 0 and h == 0), stop=(j == NT - 1 and h == 1), skip_group_check=True)
                    last.then_inc(S["fin_y"], 1)
        block = ctx.enter_context(nc.Block())

        @block.sync
        def _(e):
            sp_prologue(e)
            with e.Fori(0, B) as b:
                e.dma_start(X[:, :, :], a["L0_attn_x"][b].rearrange("(j p) c -> p j c", p=P)).then_inc(S["x_in"], 16)
                sp_l0(e, b)
                sp_l1(e, b)
                sp_f1(e, b)
                wait_alone(e, at("x", b, 3))
                e.wait_ge(S["x"], at("x", b, 3))
                e.dma_start(x_dram[b], X[:, :, :]).then_inc(S["x_saved"], 16)
                sp_l3(e, b)
                wait_alone(e, at("gate", b, 4))
                e.wait_ge(S["gate"], at("gate", b, 4))
                e.dma_start(g_dram[b], GB[:, :, :]).then_inc(S["g_saved"], 16)
                wait_alone(e, at("x_saved", b, 16))
                e.wait_ge(S["x_saved"], at("x_saved", b, 16))
            sp_final(e)

        @block.gpsimd
        def _(e):
            pool_prologue(e)
            ready(e)
            with e.Fori(0, B) as b:
                pool_norm(e, b, 0)
                pool_l0(e, b)
                pool_norm(e, b, 1)
                pool_l1(e, b)
                pool_l3(e, b)
                pool_norm(e, b, 2)
                pool_norm(e, b, 3)

        @block.scalar
        def _(e):
            act_prologue(e)
            act_late_loads(e)
            ready(e)
            with e.Fori(0, B) as b:
                act_norm(e, b, 0)
                act_l0(e, b)
                act_norm(e, b, 1)
                act_l1(e, b)
                act_f1(e, b)
                act_norm(e, b, 2)
                act_pairs(e, b, 2)
                act_norm(e, b, 3)
                act_attn(e, b, "A", act_sig3, lambda e, b: act_combine(e, b, 3))
                act_pairs(e, b, 3)
            act_final(e)

        @block.vector
        def _(e):
            dve_prologue(e)
            ready(e)
            with e.Fori(0, B) as b:
                count = [0]

                def step(ins, alone=False):
                    count[0] += 1
                    ins.then_inc(S["dve"], 1)
                    if alone:
                        wait_alone(e, at("dve", b, count[0]))
                    e.wait_ge(S["dve"], at("dve", b, count[0]))

                e.wait_ge(S["x_in"], at("x_in", b, 16))
                dve_norm(e, b, 0, step)
                dve_l0(e, b, step)
                dve_update(e, b, 0, step)
                dve_norm(e, b, 1, step)
                dve_l1(e, b, step)
                dve_f1(e, b, step)
                dve_norm(e, b, 2, step)
                dve_l2(e, b, step)
                dve_pairs(e, b, 2, step)
                dve_update(e, b, 2, step)
                dve_norm(e, b, 3, step)
                dve_l3(e, b, step)
                dve_pairs(e, b, 3, step)
            dve_final(e)

        @block.tensor
        def _(e):
            pe_prologue(e)
            ready(e)
            with e.Fori(0, B) as b:
                pe_norm(e, b, 0)
                pe_l0(e, b)
                pe_norm(e, b, 1)
                pe_l1(e, b)
                pe_f1(e, b)
                pe_norm(e, b, 2)
                pe_l2(e, b)
                pe_pairs(e, b, 2)
                pe_norm(e, b, 3)
                pe_l3(e, b)
                pe_pairs(e, b, 3)
            pe_final(e)


def kernel(**inputs):
    import concourse.bacc as _bacc
    from concourse.bass_utils import run_bass_kernel_spmd as _run

    nc = _bacc.Bacc("TRN2", target_bir_lowering=False, num_devices=1)
    arrays = {name: np.ascontiguousarray(v) for name, v in inputs.items()}
    arrays["consts"] = shape_constants()[0]
    a = {}
    for name, v in arrays.items():
        a[name] = nc.dram_tensor(f"in_{name}_dram", v.shape, mybir.dt.from_np(v.dtype), kind="ExternalInput").ap()
    out = nc.dram_tensor("out_0_dram", (B, T, C), FP32, kind="ExternalOutput").ap()
    build(nc, a, out)
    r = _run(nc, [{f"in_{name}_dram": v for name, v in arrays.items()}], core_ids=[0])
    return r.results[0]["out_0_dram"]
```
